# Optimizing a Trainium2 kernel written in Bass

```python
import numpy as np
import jax
import jax.numpy as jnp

def _softmax(x, axis=-1):
    return jax.nn.softmax(x, axis=axis)

def _gelu(x):
    return jax.nn.gelu(x, approximate=True)

def _silu(x):
    return jax.nn.silu(x)

def _sigmoid(x):
    return jax.nn.sigmoid(x)

def _layernorm(x, axis=-1, eps=1e-05):
    m = jnp.mean(x, axis=axis, keepdims=True)
    v = jnp.var(x, axis=axis, keepdims=True)
    return (x - m) / jnp.sqrt(v + eps)

def _scatter_add(tgt, idx, src, axis=0):
    return tgt.at[idx].add(src)

def _segment_sum(src, seg, n):
    return jax.ops.segment_sum(src, seg, n)
kernel_name = 'mk_gnn_preln_d1_gnn_r64_31dd4a'

def setup_inputs(seed: int=0):
    np.random.seed(seed)
    _w = jnp.asarray

    def _rec_inputs():
        import jax
        import jax.numpy as jnp
        _gk = jax.random.key(seed)
        x = -0.0005121 + 1.001 * jax.random.normal(jax.random.fold_in(_gk, 1), (100000, 32), jnp.float32)
        src = jax.random.randint(jax.random.fold_in(_gk, 2), (50000,), 0, 100000, jnp.int32)
        dst = jnp.minimum((100000 * jax.random.uniform(jax.random.fold_in(_gk, 3), (50000,)) ** 2.0).astype(jnp.int32), 99999)
        _o = jnp.argsort(dst, stable=True)
        src = src[_o]
        dst = dst[_o]
        edge_attr_2 = jax.random.uniform(jax.random.fold_in(_gk, 11), (50000, 2), jnp.float32, 0.0, 1)
        return (x, src, dst, edge_attr_2)
    x, src, dst, edge_attr_2 = _rec_inputs()

    def _L0_gnn_setup():
        import jax, jax.numpy as jnp
        import numpy as np
        N_NODES = 100000
        N_EDGES = 50000
        IN_CH = 32
        OUT_CH = 32
        DIM = 2
        KSIZE = 3

        def _basis(pseudo):
            p = jnp.clip(pseudo, 0.0, 1.0)
            grid = jnp.linspace(0.0, 1.0, KSIZE, dtype=p.dtype)
            dist = jnp.abs(p[:, :, None] - grid[None, None, :])
            b = jnp.maximum(1.0 - dist * (KSIZE - 1), 0.0)
            basis = jnp.einsum('ea,eb->eab', b[:, 0], b[:, 1])
            return basis.reshape(p.shape[0], -1)
        key = jax.random.key(seed)
        k1, k2, k3, k4, k5, k6 = jax.random.split(key, 6)
        x = jax.random.normal(k1, (N_NODES, IN_CH), dtype=jnp.float32)
        pseudo = jax.random.uniform(k2, (N_EDGES, DIM), dtype=jnp.float32)
        weight = jax.random.normal(k3, (KSIZE * KSIZE, IN_CH, OUT_CH), dtype=jnp.float32) / np.sqrt(IN_CH)
        root_w = jax.random.normal(k4, (OUT_CH, IN_CH), dtype=jnp.float32) / np.sqrt(IN_CH)
        root_b = jax.random.normal(k5, (OUT_CH,), dtype=jnp.float32) * 0.01
        edge_index = jax.random.randint(k6, (2, N_EDGES), 0, N_NODES, dtype=jnp.int64)
        return {'x': x, 'pseudo': pseudo, 'weight': weight, 'root_w': root_w, 'root_b': root_b, 'edge_index': edge_index}
    _L0_gnn_all = _L0_gnn_setup()
    _L0_gnn_in = {k: v for k, v in _L0_gnn_all.items() if k in ('weight', 'root_w', 'root_b')}
    del _L0_gnn_all
    return {'x': x, 'src': src, 'dst': dst, 'edge_attr_2': edge_attr_2, 'L0_gnn_weight': _L0_gnn_in['weight'], 'L0_gnn_root_w': _L0_gnn_in['root_w'], 'L0_gnn_root_b': _L0_gnn_in['root_b']}

def reference(x, src, dst, edge_attr_2, L0_gnn_weight, L0_gnn_root_w, L0_gnn_root_b):
    import jax
    import jax.numpy as jnp

    def _L0_gnn_ref(x, pseudo, weight, root_w, root_b, edge_index):
        import jax, jax.numpy as jnp
        import numpy as np
        N_NODES = 100000
        N_EDGES = 50000
        IN_CH = 32
        OUT_CH = 32
        DIM = 2
        KSIZE = 3

        def _basis(pseudo):
            p = jnp.clip(pseudo, 0.0, 1.0)
            grid = jnp.linspace(0.0, 1.0, KSIZE, dtype=p.dtype)
            dist = jnp.abs(p[:, :, None] - grid[None, None, :])
            b = jnp.maximum(1.0 - dist * (KSIZE - 1), 0.0)
            basis = jnp.einsum('ea,eb->eab', b[:, 0], b[:, 1])
            return basis.reshape(p.shape[0], -1)
        row, col = (edge_index[0], edge_index[1])
        basis = _basis(pseudo)
        messages = jnp.einsum('ek,ei,kio->eo', basis, x[row], weight)
        out = jnp.zeros((x.shape[0], weight.shape[2]), dtype=x.dtype).at[col].add(messages)
        degree = jnp.zeros((x.shape[0],), dtype=x.dtype).at[col].add(jnp.ones_like(col, dtype=x.dtype))
        out = out / jnp.maximum(degree, 1.0)[:, None]
        out = out + x @ root_w.T + root_b
        return out
    edge_index = jnp.stack([src, dst])
    h = jnp.maximum(_layernorm(x, axis=-1), 0.0)
    x = x + _L0_gnn_ref(h, edge_attr_2, L0_gnn_weight, L0_gnn_root_w, L0_gnn_root_b, edge_index)
    return x

_drawn_inputs = setup_inputs


def setup_inputs(seed=0):
    import zlib

    import numpy as np

    out = dict(_drawn_inputs(seed))
    spreads = {}
    factors = {'L0_gnn_root_b': 7.219}
    for name, (base, spread) in spreads.items():
        noise = np.random.default_rng([zlib.crc32(name.encode()), seed]).standard_normal(out[name].shape)
        drawn = base * np.exp(spread * noise) if base else spread * noise
        out[name] = jnp.asarray(drawn.astype(out[name].dtype))
    for name, factor in factors.items():
        out[name] = (out[name] * factor).astype(out[name].dtype)
    return out
```

```python
from contextlib import ExitStack

import concourse.bass as bass
from concourse import mybir

F32 = mybir.dt.float32
I32 = mybir.dt.int32
ALU = mybir.AluOpType
ACT = mybir.ActivationFunctionType
AX_X = mybir.AxisListType.X
ds = bass.ds

P = 128
WIN = 4
GT_TILES = 4
XG_SLOTS = 4
PAD_NODE = 1 << 20
EPS = 1e-5
TABLE_STEPS = 7
SPREAD_BANK = (0, 1, 2, 0)
BANK_LAG = (1, 4, 4, 3)


def build_gnn(nc, x, src, dst, edge_attr, weight, root_w, root_b, out):
    N, C = x.shape
    E = src.shape[0]
    K = weight.shape[0]
    KS = 3
    D = edge_attr.shape[1]
    assert C == 32 and K == KS * KS and D == 2
    CW = C + 1
    J = 2
    SB = P * J
    NSB = -(-N // SB)
    BW = J * CW
    WB = WIN * J
    WC = WB * CW
    GRP = -(-(-(-E // P)) // GT_TILES)
    TILES = GRP * GT_TILES
    RC = 4
    RT = TILES // RC
    full_tiles, tail_edges = divmod(E, P)
    KG = 3
    NKG = K // KG
    assert TILES == RC * RT and (GRP - 2) % 4 == 0 and full_tiles - (RC - 1) * RT == 96
    LOOPS = (GRP - 2) // 4

    CS = 8
    CB = CS * J
    CC = CB * C
    NCH = -(-NSB // CS)
    AGG_SB = max(NSB + WIN - 1, NCH * CS)
    XBUF = 4
    full_sb, tail_nodes = divmod(N, SB)
    tail_sb = full_sb - (NCH - 1) * CS
    QUADS = CB // 4

    with ExitStack() as ctx:
        def sb(name, shape, dt=F32):
            return ctx.enter_context(nc.sbuf_tensor(name, shape, dt))

        def sem(name):
            return ctx.enter_context(nc.semaphore(name))

        bank = [ctx.enter_context(nc.psum_tensor(f"bank{i}", [P, 512], F32)) for i in range(8)]

        agg = sb("agg", [P, AGG_SB * BW])
        ident = sb("ident", [P, P])
        iota_i = sb("iota_i", [P, P], I32)
        iota_row = sb("iota_row", [P, P])
        col_i = sb("col_i", [P, 1], I32)
        col_f = sb("col_f", [P, 1])
        eps = sb("eps", [P, 1])
        src_idx = sb("src_idx", [P, TILES], I32)
        plane = sb("plane", [P, TILES])
        rel = sb("rel", [P, TILES])
        basis = sb("basis", [P, TILES, K])
        mask = sb("mask", [P, TILES, WB])
        base_row = sb("base_row", [1, TILES], I32)
        sweeps_i = sb("sweeps_i", [1, 1], I32)
        w_sb = sb("w_sb", [KG * C, NKG, C])
        root_bd = sb("root_bd", [P, P])
        root_t = sb("root_t", [P, P])
        center = sb("center", [P, P])
        quarter = sb("quarter", [P, 4])
        bias = sb("bias", [P, C])

        consts_made = sem("consts_made")
        pool_consts = sem("pool_consts")
        rows_padded = sem("rows_padded")
        rows_in = sem("rows_in")
        weights_in = sem("weights_in")
        root_in = sem("root_in")
        step_done = sem("step_done")
        tables_up = sem("tables_up")
        range_up = sem("range_up")
        root_up = sem("root_up")

        with ExitStack() as st:
            def tmp(name, shape, dt=F32):
                return st.enter_context(nc.sbuf_tensor(name, shape, dt))
            src_r = tmp("src_r", [RT, RC, P], I32)
            dst_r = tmp("dst_r", [RT, RC, P], I32)
            attr_r = tmp("attr_r", [RT, RC, P * D])
            src_f = tmp("src_f", [RT, RC, P])
            sb_i = tmp("sb_i", [RT, RC, P], I32)
            pl_i = tmp("pl_i", [RT, RC, P], I32)
            j_i = tmp("j_i", [RT, RC, P], I32)
            sb_f = tmp("sb_f", [RT, RC, P])
            sb_m = tmp("sb_m", [RT, RC, P])
            pl_f = tmp("pl_f", [RT, RC, P])
            j_f = tmp("j_f", [RT, RC, P])
            blk_f = tmp("blk_f", [RT, RC, P])
            rel_f = tmp("rel_f", [RT, RC, P])
            low = tmp("low", [RT, RC])
            low_c = tmp("low_c", [RT, RC])
            high = tmp("high", [RT, RC])
            span = tmp("span", [RT, RC])
            widest = tmp("widest", [RT, 1])
            widest_1 = tmp("widest_1", [1, 1])
            span_i = tmp("span_i", [1, 1], I32)
            span_s = tmp("span_s", [1, 1], I32)
            span_sf = tmp("span_sf", [1, 1])
            pc = tmp("pc", [P, D, TILES])
            pd = tmp("pd", [P, D, TILES])
            pe_ = tmp("pe", [P, D, TILES])
            hat = tmp("hat", [P, D, KS, TILES])
            block = st.enter_context(nc.Block())

            def dram_rows(a, width):
                n = (RC - 1) * RT * P
                if width == 1:
                    return (a[0:n].rearrange("(c r p) -> r c p", r=RT, p=P),
                            a[n:full_tiles * P].rearrange("(r p) -> r p", p=P),
                            a[full_tiles * P:E].rearrange("(r p) -> r p", r=1))
                return (a[0:n, :].rearrange("(c r p) d -> r c (p d)", r=RT, p=P),
                        a[n:full_tiles * P, :].rearrange("(r p) d -> r (p d)", p=P),
                        a[full_tiles * P:E, :].rearrange("(r p) d -> r (p d)", r=1))

            @block.sync
            def _(sp):
                sp.wait_ge(rows_padded, 3)
                for table, a, width in ((dst_r, dst, 1), (src_r, src, 1), (attr_r, edge_attr, D)):
                    most, rest, last = dram_rows(a, width)
                    sp.dma_start(table[:, 0:RC - 1, :], most).then_inc(rows_in, 16)
                    sp.dma_start(table[0:96, RC - 1, :], rest).then_inc(rows_in, 16)
                    sp.dma_start(table[96:97, RC - 1, 0:tail_edges * width], last).then_inc(rows_in, 16)

            @block.scalar
            def _(act):
                act.dma_start(w_sb[:], weight.rearrange("(g k) i o -> (k i) g o", k=KG)).then_inc(weights_in, 16)
                act.dma_start(bias[:], root_b.rearrange("(a c) -> a c", a=1).broadcast_to([P, C])).then_inc(weights_in, 16)
                act.wait_ge(consts_made, 3)
                for b in range(4):
                    act.dma_start(root_bd[b * C:(b + 1) * C, b * C:(b + 1) * C], root_w).then_inc(root_in, 16)

            @block.gpsimd
            def _(pool):
                nc.gpsimd.iota(iota_i[:], pattern=[[1, P]], base=0, channel_multiplier=0).then_inc(pool_consts, 1)
                nc.gpsimd.iota(col_i[:], pattern=[[1, 1]], base=0, channel_multiplier=1).then_inc(pool_consts, 1)

            @block.vector
            def _(dve):
                done = [0]

                def step(ins):
                    done[0] += 1
                    ins.then_inc(step_done, 1)
                    dve.wait_ge(step_done, done[0])

                for table, fill in ((dst_r, PAD_NODE), (src_r, 0), (attr_r, 0)):
                    nc.vector.memset(table[96:RT, RC - 1, :], fill).then_inc(rows_padded, 1)
                nc.vector.memset(center[:], 0.0).then_inc(consts_made, 1)
                nc.vector.memset(quarter[:], 0.0).then_inc(consts_made, 1)
                nc.vector.memset(root_bd[:], 0.0).then_inc(consts_made, 1)
                nc.vector.memset(eps[:], EPS).then_inc(consts_made, 1)
                dve.wait_ge(consts_made, 4)
                for b in range(4):
                    rows = slice(b * C, (b + 1) * C)
                    nc.vector.memset(center[rows, rows], -1.0 / C).then_inc(consts_made, 1)
                    nc.vector.memset(quarter[rows, b:b + 1], 1.0 / C).then_inc(consts_made, 1)
                dve.wait_ge(pool_consts, 2)
                nc.vector.tensor_copy(iota_row[:], iota_i[:]).then_inc(consts_made, 1)
                nc.vector.tensor_copy(col_f[:], col_i[:]).then_inc(consts_made, 1)
                dve.wait_ge(consts_made, 14)
                nc.vector.tensor_scalar(ident[:], iota_row[:], col_f[:, 0:1], None, ALU.is_equal).then_inc(consts_made, 1)
                dve.wait_ge(consts_made, 15)
                step(nc.vector.tensor_tensor(center[:], center[:], ident[:], ALU.add))
                dve.wait_ge(rows_in, 9 * 16)
                nc.vector.tensor_scalar(sb_i[:], dst_r[:], 8, None, ALU.logical_shift_right)
                nc.vector.tensor_scalar(j_i[:], dst_r[:], 1, None, ALU.bitwise_and)
                nc.vector.tensor_copy(src_f[:], src_r[:])
                step(nc.vector.tensor_scalar(pl_i[:], dst_r[:], 1, 127, ALU.logical_shift_right, ALU.bitwise_and))
                nc.vector.tensor_copy(pl_f[:], pl_i[:])
                nc.vector.tensor_copy(j_f[:], j_i[:])
                step(nc.vector.tensor_copy(sb_f[:], sb_i[:]))
                nc.vector.scalar_tensor_tensor(out=sb_m[:], in0=sb_f[:], scalar=float(PAD_NODE // SB), in1=sb_f[:],
                                               op0=ALU.is_lt, op1=ALU.mult)
                nc.vector.scalar_tensor_tensor(out=blk_f[:], in0=sb_f[:], scalar=float(J), in1=j_f[:],
                                               op0=ALU.mult, op1=ALU.add)
                step(nc.vector.tensor_reduce(low[:], sb_f[:], AX_X, ALU.min))
                nc.vector.tensor_reduce(high[:], sb_m[:], AX_X, ALU.max)
                step(nc.vector.tensor_scalar(low_c[:], low[:], float(NSB - 1), None, ALU.min))
                nc.vector.scalar_tensor_tensor(out=rel_f[:], in0=low_c[:].unsqueeze(2).broadcast_to([RT, RC, P]),
                                               scalar=-float(J), in1=blk_f[:], op0=ALU.mult, op1=ALU.add)
                step(nc.vector.tensor_tensor(span[:], high[:], low_c[:], ALU.subtract))
                step(nc.vector.tensor_reduce(widest[:], span[:], AX_X, ALU.max))
                done_tables = done[0]
                assert done_tables == TABLE_STEPS
                dve.wait_ge(range_up, 1)
                nc.vector.tensor_copy(base_row[:], bank[5][0:1, 0:TILES])
                step(nc.vector.tensor_reduce(widest_1[:], bank[4][0:1, 0:RT], AX_X, ALU.max))
                step(nc.vector.tensor_copy(span_i[:], widest_1[:]))
                step(nc.vector.tensor_scalar(span_s[:], span_i[:], WIN.bit_length() - 1, None, ALU.arith_shift_right))
                step(nc.vector.tensor_copy(span_sf[:], span_s[:]))
                step(nc.vector.tensor_scalar(sweeps_i[:], span_sf[:], 1.0, None, ALU.add))
                dve.wait_ge(tables_up, 5)
                nc.vector.tensor_copy(src_idx[:], bank[0][:, 0:TILES])
                nc.vector.tensor_copy(plane[:], bank[1][:, 0:TILES])
                nc.vector.tensor_copy(rel[:], bank[2][:, 0:TILES])
                for d in range(D):
                    nc.vector.tensor_scalar(pc[:, d, :], bank[(6, 7)[d]][:, 0:TILES], 0.0, 1.0, ALU.max, ALU.min)
                dve.wait_ge(root_up, 1)
                step(nc.vector.tensor_copy(root_t[:], bank[3][:, 0:P]))
                for a in range(KS):
                    grid = a / (KS - 1)
                    step(nc.vector.tensor_scalar(pd[:], pc[:], grid, float(KS - 1), ALU.subtract, ALU.mult))
                    step(nc.vector.tensor_scalar(pe_[:], pd[:], -1.0, 1.0, ALU.mult, ALU.add))
                    step(nc.vector.scalar_tensor_tensor(out=pd[:], in0=pd[:], scalar=1.0, in1=pe_[:],
                                                        op0=ALU.add, op1=ALU.min))
                    step(nc.vector.tensor_scalar(hat[:, :, a, :], pd[:], 0.0, None, ALU.max))
                for a in range(KS):
                    for b in range(KS):
                        nc.vector.tensor_tensor(basis[:, :, a * KS + b], hat[:, 0, a, :], hat[:, 1, b, :],
                                                ALU.mult).then_inc(step_done, 1)
                done[0] += K
                nc.vector.memset(agg[:], 0.0).then_inc(step_done, 1)
                done[0] += 1
                dve.wait_ge(step_done, done[0])

            @block.tensor
            def _(pe):
                pe.wait_ge(consts_made, 15)
                pe.wait_ge(root_in, 64)
                nc.tensor.transpose(bank[3][:, 0:P], root_bd[:], ident[:]).then_inc(root_up, 1)
                pe.wait_ge(rows_in, 9 * 16)
                for d in range(D):
                    for c in range(RC):
                        last = nc.tensor.transpose(bank[(6, 7)[d]][:, c * RT:(c + 1) * RT],
                                                   attr_r[:, c, :].rearrange("r (p d) -> r p d", d=D)[:, :, d],
                                                   ident[0:RT, 0:RT])
                    last.then_inc(tables_up, 1)
                pe.wait_ge(step_done, TABLE_STEPS)
                for i, table in enumerate((src_f, pl_f, rel_f)):
                    for c in range(RC):
                        last = nc.tensor.transpose(bank[i][:, c * RT:(c + 1) * RT], table[:, c, :], ident[0:RT, 0:RT])
                    last.then_inc(tables_up, 1)
                for c in range(RC):
                    nc.tensor.transpose(bank[5][0:1, c * RT:(c + 1) * RT], low_c[:, c:c + 1], ident[0:RT, 0:RT])
                nc.tensor.transpose(bank[4][0:1, 0:RT], widest[:], ident[0:RT, 0:RT]).then_inc(range_up, 1)

        with ExitStack() as st:
            def tmp(name, shape, dt=F32):
                return st.enter_context(nc.sbuf_tensor(name, shape, dt))
            idx_slot = [tmp(f"idx_slot{s}", [P, GT_TILES], I32) for s in range(XG_SLOTS)]
            xg = [tmp(f"xg{s}", [P, GT_TILES, C]) for s in range(XG_SLOTS)]
            xc = tmp("xc", [P, GT_TILES, C])
            xr = tmp("xr", [P, GT_TILES, C])
            sq = tmp("sq", [P, GT_TILES, C])
            row_sum = tmp("row_sum", [P, GT_TILES])
            sq_sum = tmp("sq_sum", [P, GT_TILES])
            std = tmp("std", [P, GT_TILES])
            rstd = tmp("rstd", [P, GT_TILES])
            scaled = tmp("scaled", [P, GT_TILES, K])
            spread = [tmp(f"spread{s}", [P, GT_TILES, K, C]) for s in range(2)]
            spread_t = tmp("spread_t", [KG * C, GT_TILES, NKG, P])
            msg = [tmp(f"msg{s}", [P, GT_TILES, CW]) for s in range(2)]
            onehot = [tmp(f"onehot{s}", [P, GT_TILES, P]) for s in range(2)]
            placed = [tmp(f"placed{s}", [P, GT_TILES, WB, CW]) for s in range(2)]
            ps_spread = bank[0:3]
            ps_msg = bank[3]
            ps_win = bank[4:8]

            S = {n: sem(n) for n in (
                "idx_ready", "sum_done", "xc_done", "sq_done", "relu_done", "sqsum_done", "std_done",
                "rstd_done", "scaled_done", "spread_done", "turned", "turned_out", "msg_made", "msg_out",
                "onehot_done", "placed_done", "win_made", "win_added", "ones_set", "mask_done", "moved_on")}
            landed = [sem(f"landed{s}") for s in range(XG_SLOTS)]
            sweep_sems = list(S.values()) + landed

            sweeps = nc.values_load(sweeps_i[0:1, 0:1], min_val=1, max_val=-(-NSB // WIN))
            with nc.Fori(0, sweeps):
                with nc.Block() as block:
                    def run_groups(eng, step, first, last=None):
                        for g in range(first):
                            step(g, g // 4, g % 4)
                        with eng.Fori(0, (GRP - first) // 4) as i:
                            for u in range(4):
                                g = i * 4 + (first + u)
                                step(g, i + (first + u) // 4, (first + u) % 4)
                        if last is not None:
                            last()

                    @block.gpsimd
                    def _(pool):
                        def step(g, turn, slot):
                            pool.wait_ge(S["idx_ready"], g + 1)
                            pool.nop(nofuse=True)
                            for t in range(GT_TILES):
                                nc.gpsimd.indirect_dma_start(
                                    out=xg[slot][:, t, :], out_offset=None, in_=x,
                                    in_offset=bass.IndirectOffsetOnAxis(idx_slot[slot][:, t:t + 1], 0),
                                ).then_inc(landed[slot], 16)
                        run_groups(pool, step, 2)

                    @block.scalar
                    def _(act):
                        def give_indices(g, slot):
                            at = g * GT_TILES
                            piece = src_idx[:, at:at + GT_TILES] if isinstance(g, int) else src_idx[:, ds(at, GT_TILES)]
                            nc.scalar.copy(idx_slot[slot][:], piece).then_inc(S["idx_ready"], 1)

                        for s in range(XG_SLOTS):
                            give_indices(s, s)

                        def body(g, turn, slot, more=True):
                            act.wait_ge(S["xc_done"], g + 1)
                            nc.scalar.activation(sq[:], xc[:], ACT.Square).then_inc(S["sq_done"], 1)
                            if more:
                                give_indices(g + XG_SLOTS, slot)
                            if not isinstance(g, int) or g:
                                act.wait_ge(S["spread_done"], g)
                            nc.scalar.activation(xr[:], xc[:], ACT.Relu).then_inc(S["relu_done"], 1)
                            act.wait_ge(S["sqsum_done"], g + 1)
                            nc.scalar.activation(std[:], sq_sum[:], ACT.Sqrt, bias=eps[:, 0:1],
                                                 scale=1.0 / C).then_inc(S["std_done"], 1)
                            for t in range(GT_TILES):
                                act.wait_ge(S["turned"], g * GT_TILES + (t + 1))
                                if not isinstance(g, int) or g:
                                    if t == 0:
                                        act.wait_ge(S["msg_made"], g)
                                nc.scalar.copy(spread_t[:, t, :, :],
                                               ps_spread_of(slot, t).rearrange("p (g e) -> p g e", g=NKG)
                                               ).then_inc(S["turned_out"], 1)
                            act.wait_ge(S["msg_made"], g + 1)
                            act.wait_ge(S["ones_set"], 2)
                            if not isinstance(g, int) or g >= 2:
                                act.wait_ge(S["placed_done"], g - 1)
                            nc.scalar.copy(msg[slot % 2][:, :, 0:C],
                                           ps_msg[:, 0:GT_TILES * C].rearrange("p (t c) -> p t c", t=GT_TILES)
                                           ).then_inc(S["msg_out"], 1)

                        def ps_spread_of(slot, t):
                            return bank[SPREAD_BANK[t]][0:KG * C, 0:NKG * P]

                        body(0, 0, 0)
                        body(1, 0, 1)
                        with act.Fori(0, LOOPS - 1) as i:
                            for u in range(4):
                                body(i * 4 + (2 + u), i + (2 + u) // 4, (2 + u) % 4)
                        for g in range(GRP - 4, GRP):
                            body(g, g // 4, g % 4, more=False)

                    @block.vector
                    def _(dve):
                        for s in range(2):
                            nc.vector.memset(msg[s][:, :, C:CW], 1.0).then_inc(S["ones_set"], 1)
                        nc.vector.tensor_tensor(
                            mask[:], rel[:].unsqueeze(2).broadcast_to([P, TILES, WB]),
                            iota_row[:, 0:WB].unsqueeze(1).broadcast_to([P, TILES, WB]),
                            ALU.is_equal).then_inc(S["mask_done"], 1)

                        def center_rows(g, turn, slot):
                            dve.wait_ge(landed[slot], turn * (16 * GT_TILES) + 16 * GT_TILES)
                            nc.vector.tensor_reduce(row_sum[:], xg[slot][:], AX_X, ALU.add).then_inc(S["sum_done"], 1)
                            dve.wait_ge(S["sum_done"], g + 1)
                            if not isinstance(g, int) or g:
                                dve.wait_ge(S["relu_done"], g)
                            ins = nc.vector.scalar_tensor_tensor(
                                out=xc[:], in0=row_sum[:].unsqueeze(2).broadcast_to([P, GT_TILES, C]),
                                scalar=-1.0 / C, in1=xg[slot][:], op0=ALU.mult, op1=ALU.add)
                            ins.then_inc(S["xc_done"], 1)

                        def one_hot(g, slot):
                            if not isinstance(g, int) or g >= 2:
                                dve.wait_ge(S["win_made"], (g - 1) * GT_TILES)
                            at = g * GT_TILES
                            pl = plane[:, at:at + GT_TILES] if isinstance(g, int) else plane[:, ds(at, GT_TILES)]
                            nc.vector.tensor_tensor(
                                onehot[slot % 2][:], iota_row[:].unsqueeze(1).broadcast_to([P, GT_TILES, P]),
                                pl.unsqueeze(2).broadcast_to([P, GT_TILES, P]), ALU.is_equal).then_inc(S["onehot_done"], 1)

                        def place(g, slot):
                            dve.wait_ge(S["msg_out"], g + 1)
                            dve.wait_ge(S["mask_done"], 1)
                            at = g * GT_TILES
                            m = mask[:, at:at + GT_TILES, :] if isinstance(g, int) else mask[:, ds(at, GT_TILES), :]
                            nc.vector.tensor_tensor(
                                placed[slot % 2][:], m.unsqueeze(3).broadcast_to([P, GT_TILES, WB, CW]),
                                msg[slot % 2][:].unsqueeze(2).broadcast_to([P, GT_TILES, WB, CW]),
                                ALU.mult).then_inc(S["placed_done"], 1)

                        def spread_rows(g, slot):
                            dve.wait_ge(S["sq_done"], g + 1)
                            nc.vector.tensor_reduce(sq_sum[:], sq[:], AX_X, ALU.add).then_inc(S["sqsum_done"], 1)
                            dve.wait_ge(S["std_done"], g + 1)
                            nc.vector.reciprocal(rstd[:], std[:]).then_inc(S["rstd_done"], 1)
                            dve.wait_ge(S["rstd_done"], g + 1)
                            at = g * GT_TILES
                            b = basis[:, at:at + GT_TILES, :] if isinstance(g, int) else basis[:, ds(at, GT_TILES), :]
                            nc.vector.tensor_tensor(scaled[:], b, rstd[:].unsqueeze(2).broadcast_to([P, GT_TILES, K]),
                                                    ALU.mult).then_inc(S["scaled_done"], 1)
                            dve.wait_ge(S["scaled_done"], g + 1)
                            if not isinstance(g, int) or g >= 2:
                                dve.wait_ge(S["turned"], (g - 1) * GT_TILES)
                            dve.wait_ge(S["relu_done"], g + 1)
                            nc.vector.tensor_tensor(
                                spread[slot % 2][:], xr[:].unsqueeze(2).broadcast_to([P, GT_TILES, K, C]),
                                scaled[:].unsqueeze(3).broadcast_to([P, GT_TILES, K, C]), ALU.mult).then_inc(S["spread_done"], 1)

                        def add_windows(g, slot):
                            for t in range(GT_TILES):
                                at = g * GT_TILES + t
                                first = dve.value_load(
                                    base_row[0:1, at:at + 1] if isinstance(g, int) else base_row[0:1, ds(at, 1)],
                                    min_val=0, max_val=NSB - 1)
                                dve.wait_ge(S["win_made"], at + 1)
                                if not isinstance(at, int) or at:
                                    dve.wait_ge(S["win_added"], at)
                                a = agg[:, ds(first * BW, WC)]
                                nc.vector.tensor_tensor(a, a, ps_win[t][:, 0:WC], ALU.add).then_inc(S["win_added"], 1)

                        def body(g, turn, slot):
                            center_rows(g, turn, slot)
                            one_hot(g - 1, (slot - 1) % 4)
                            place(g - 1, (slot - 1) % 4)
                            spread_rows(g, slot)
                            add_windows(g - 1, (slot - 1) % 4)

                        center_rows(0, 0, 0)
                        spread_rows(0, 0)
                        body(1, 0, 1)
                        with dve.Fori(0, LOOPS) as i:
                            for u in range(4):
                                body(i * 4 + (2 + u), i + (2 + u) // 4, (2 + u) % 4)
                        one_hot(GRP - 1, (GRP - 1) % 4)
                        place(GRP - 1, (GRP - 1) % 4)
                        add_windows(GRP - 1, (GRP - 1) % 4)
                        nc.vector.tensor_scalar(rel[:], rel[:], -float(WB), None, ALU.add).then_inc(S["moved_on"], 1)
                        nc.vector.tensor_scalar(base_row[:], base_row[:], float(WIN), float(NSB - 1),
                                                ALU.add, ALU.min).then_inc(S["moved_on"], 1)
                        dve.wait_ge(S["moved_on"], 2)

                    @block.tensor
                    def _(pe):
                        def turn_spread(g, slot):
                            for t in range(GT_TILES):
                                if t == 0:
                                    pe.wait_ge(S["spread_done"], g + 1)
                                first_use = isinstance(g, int) and g == 0 and t < 3
                                if not first_use:
                                    pe.wait_ge(S["turned_out"], g * GT_TILES + t - BANK_LAG[t] + 1)
                                for k in range(NKG):
                                    last = nc.tensor.transpose(
                                        bank[SPREAD_BANK[t]][0:KG * C, k * P:(k + 1) * P],
                                        spread[slot % 2][:, t, k * KG:(k + 1) * KG, :].rearrange("p k c -> p (k c)"),
                                        ident[:])
                                last.then_inc(S["turned"], 1)

                        def make_messages(g, slot):
                            if not isinstance(g, int) or g:
                                pe.wait_ge(S["msg_out"], g)
                            for t in range(GT_TILES):
                                pe.wait_ge(S["turned_out"], g * GT_TILES + (t + 1))
                                for k in range(NKG):
                                    last = nc.tensor.matmul(ps_msg[:, t * C:(t + 1) * C], spread_t[:, t, k, :],
                                                            w_sb[:, k, :], start=(k == 0), stop=(k == NKG - 1))
                            last.then_inc(S["msg_made"], 1)

                        def make_windows(g, slot):
                            pe.wait_ge(S["onehot_done"], g + 1)
                            pe.wait_ge(S["placed_done"], g + 1)
                            for t in range(GT_TILES):
                                if not isinstance(g, int) or g:
                                    pe.wait_ge(S["win_added"], (g - 1) * GT_TILES + (t + 1))
                                nc.tensor.matmul(ps_win[t][:, 0:WC], onehot[slot % 2][:, t, :],
                                                 placed[slot % 2][:, t, :, :].rearrange("p w c -> p (w c)"),
                                                 start=True, stop=True).then_inc(S["win_made"], 1)

                        def body(g, turn, slot):
                            make_windows(g - 1, (slot - 1) % 4)
                            turn_spread(g, slot)
                            make_messages(g, slot)

                        pe.wait_ge(weights_in, 32)
                        turn_spread(0, 0)
                        make_messages(0, 0)
                        body(1, 0, 1)
                        with pe.Fori(0, LOOPS) as i:
                            for u in range(4):
                                body(i * 4 + (2 + u), i + (2 + u) // 4, (2 + u) % 4)
                        make_windows(GRP - 1, (GRP - 1) % 4)

                nums = sorted(s.num for s in sweep_sems)
                assert nums == list(range(nums[0], nums[0] + len(nums)))
                nc.gpsimd.sem_clear(range(nums[0], nums[-1] + 1))
                nc.all_engine_barrier()

        with ExitStack() as st:
            def tmp(name, shape, dt=F32):
                return st.enter_context(nc.sbuf_tensor(name, shape, dt))
            xin = tmp("xin", [P, XBUF, CC])
            xb = tmp("xb", [P, 2, CC])
            x_t = tmp("x_t", [P, 2, CC])
            relu_t = tmp("relu_t", [P, 2, CC])
            sq_t = tmp("sq_t", [P, 2, CC])
            nstd = tmp("nstd", [P, 2, CB])
            nrstd = tmp("nrstd", [P, 2, CB])
            deg = tmp("deg", [P, 2, CB])
            rdeg = tmp("rdeg", [P, 2, CB])
            mean_msg = tmp("mean_msg", [P, 2, CC])
            part = tmp("part", [P, 2, CC])
            part2 = tmp("part2", [P, 2, CC])
            res = tmp("res", [P, 2, CC])
            ps_xt, ps_xc, ps_root, ps_var = bank[0:2], bank[2:4], bank[4:6], bank[6:8]
            x_in = [sem(f"x_in{s}") for s in range(XBUF)]
            stored = [sem(f"stored{s}") for s in range(2)]
            T = {n: sem("n_" + n) for n in (
                "xt", "xt_out", "xc", "relu", "sq", "var", "root", "std", "rstd", "xb", "deg", "rdeg",
                "mean", "part", "part2", "res")}
            assert (NCH - 5) % 4 == 0
            NL = (NCH - 5) // 4

            def chunk_view(a):
                return a[0:full_sb * SB, :].rearrange("(s p j) c -> p s (j c)", p=P, j=J)

            def tail_view(a):
                return a[full_sb * SB:N, :].rearrange("(p j) c -> p (j c)", j=J)

            block = st.enter_context(nc.Block())

            def run_chunks(eng, step):
                for c in range(4):
                    step(c, 0, c)
                with eng.Fori(0, NL) as i:
                    for u in range(4):
                        step(i * 4 + (4 + u), i + 1, u)
                step(NCH - 1, NL + 1, 0)

            def cut(a, c, n):
                return a[:, c * n:(c + 1) * n] if isinstance(c, int) else a[:, ds(c * n, n)]

            def first_is(c, n):
                return isinstance(c, int) and c < n

            @block.sync
            def _(sp):
                views, out_views = chunk_view(x), chunk_view(out)
                LAST = NCH - 1

                def rows(view, c):
                    return view[:, c * CS:(c + 1) * CS, :] if isinstance(c, int) else view[:, ds(c * CS, CS), :]

                def load(c, slot):
                    if not first_is(c, XBUF):
                        sp.wait_ge(T["xt"], c - (XBUF - 1))
                        sp.wait_ge(T["xb"], c - (XBUF - 1))
                    if isinstance(c, int) and c == LAST:
                        sp.dma_start(xin[:, slot, 0:tail_sb * J * C].rearrange("p (s e) -> p s e", s=tail_sb),
                                     views[:, c * CS:c * CS + tail_sb, :]).then_inc(x_in[slot], 16)
                        sp.dma_start(xin[0:tail_nodes // J, slot, tail_sb * J * C:(tail_sb + 1) * J * C],
                                     tail_view(x)).then_inc(x_in[slot], 16)
                    else:
                        sp.dma_start(xin[:, slot, :].rearrange("p (s e) -> p s e", s=CS),
                                     rows(views, c)).then_inc(x_in[slot], 16)

                def store(c, h):
                    sp.wait_ge(T["res"], c + 1)
                    if isinstance(c, int) and c == LAST:
                        sp.dma_start(views_tail(out_views), res[:, h, 0:tail_sb * J * C].rearrange(
                            "p (s e) -> p s e", s=tail_sb)).then_inc(stored[h], 16)
                        sp.dma_start(tail_view(out), res[0:tail_nodes // J, h, tail_sb * J * C:(tail_sb + 1) * J * C]
                                     ).then_inc(stored[h], 16)
                    else:
                        sp.dma_start(rows(out_views, c), res[:, h, :].rearrange("p (s e) -> p s e", s=CS)
                                     ).then_inc(stored[h], 16)

                def views_tail(view):
                    return view[:, LAST * CS:LAST * CS + tail_sb, :]

                for c in range(XBUF):
                    load(c, c)
                with sp.Fori(0, (NCH - 5) // 4) as i:
                    for u in range(4):
                        load(i * 4 + (4 + u), u)
                        store(i * 4 + u, u % 2)
                load(LAST, LAST % XBUF)
                for c in range(NCH - 5, NCH):
                    store(c, c % 2)
                sp.wait_ge(stored[0], 16 * (NCH // 2) + 32)
                sp.wait_ge(stored[1], 16 * (NCH // 2))

            def landed_count(c, turn):
                return turn * 16 + (32 if first_is(c, NCH) and c == NCH - 1 else 16)

            @block.gpsimd
            def _(pool):
                def step(c, turn, slot):
                    h = slot % 2
                    pool.wait_ge(x_in[slot], landed_count(c, turn))
                    if not first_is(c, 2):
                        pool.wait_ge(T["part2"], c - 1)
                    nc.gpsimd.tensor_tensor(xb[:, h, :].rearrange("p (b c) -> p b c", c=C),
                                            xin[:, slot, :].rearrange("p (b c) -> p b c", c=C),
                                            bias[:].unsqueeze(1).broadcast_to([P, CB, C]), ALU.add).then_inc(T["xb"], 1)
                run_chunks(pool, step)

            @block.tensor
            def _(pe):
                def turn_in(c, turn, slot):
                    h = slot % 2
                    pe.wait_ge(x_in[slot], landed_count(c, turn))
                    if not first_is(c, 2):
                        pe.wait_ge(T["xt_out"], c - 1)
                    for q in range(QUADS):
                        last = nc.tensor.transpose(ps_xt[h][:, q * P:(q + 1) * P], xin[:, slot, q * P:(q + 1) * P], ident[:])
                    last.then_inc(T["xt"], 1)

                def centre(c, turn, slot):
                    h = slot % 2
                    pe.wait_ge(T["xt_out"], c + 1)
                    if not first_is(c, 2):
                        pe.wait_ge(T["relu"], c - 1)
                        pe.wait_ge(T["sq"], c - 1)
                    nc.tensor.matmul(ps_xc[h][:], center[:], x_t[:, h, :], start=True, stop=True).then_inc(T["xc"], 1)

                def products(c, turn, slot):
                    h = slot % 2
                    pe.wait_ge(T["sq"], c + 1)
                    if not first_is(c, 2):
                        pe.wait_ge(T["std"], c - 1)
                    for q in range(QUADS):
                        last = nc.tensor.matmul(ps_var[h][:, q * 4:(q + 1) * 4], sq_t[:, h, q * P:(q + 1) * P], quarter[:],
                                                start=True, stop=True)
                    last.then_inc(T["var"], 1)
                    pe.wait_ge(T["relu"], c + 1)
                    if not first_is(c, 2):
                        pe.wait_ge(T["part"], c - 1)
                    for q in range(QUADS):
                        last = nc.tensor.matmul(ps_root[h][:, q * P:(q + 1) * P], relu_t[:, h, q * P:(q + 1) * P], root_t[:],
                                                start=True, stop=True)
                    last.then_inc(T["root"], 1)

                def step(c, turn, slot):
                    turn_in(c, turn, slot)
                    if not first_is(c, 1):
                        products(c - 1, turn, (slot - 1) % 4)
                    centre(c, turn, slot)
                run_chunks(pe, step)
                products(NCH - 1, 0, 0)

            @block.scalar
            def _(act):
                def step(c, turn, slot):
                    h = slot % 2
                    act.wait_ge(T["xt"], c + 1)
                    if not first_is(c, 2):
                        act.wait_ge(T["xc"], c - 1)
                    nc.scalar.copy(x_t[:, h, :], ps_xt[h][:]).then_inc(T["xt_out"], 1)
                    act.wait_ge(T["xc"], c + 1)
                    if not first_is(c, 2):
                        act.wait_ge(T["var"], c - 1)
                        act.wait_ge(T["root"], c - 1)
                    nc.scalar.activation(sq_t[:, h, :], ps_xc[h][:], ACT.Square).then_inc(T["sq"], 1)
                    nc.scalar.activation(relu_t[:, h, :], ps_xc[h][:], ACT.Relu).then_inc(T["relu"], 1)
                    if not first_is(c, 1):
                        std_of(c - 1, 1 - h)

                def std_of(c, h):
                    act.wait_ge(T["var"], c + 1)
                    if not first_is(c, 2):
                        act.wait_ge(T["rstd"], c - 1)
                    nc.scalar.activation(nstd[:, h, :], ps_var[h][:, 0:CB], ACT.Sqrt, bias=eps[:, 0:1]).then_inc(T["std"], 1)
                run_chunks(act, step)
                std_of(NCH - 1, (NCH - 1) % 2)

            @block.vector
            def _(dve):
                def combine(c, h):
                    blocks = cut(agg[:].rearrange("p (b e) -> p b e", e=CW), c, CB)
                    cols = lambda a: a[:, h, :].rearrange("p (b c) -> p b c", c=C)
                    wide = lambda a: a[:, h, :].unsqueeze(2).broadcast_to([P, CB, C])
                    nc.vector.tensor_scalar(deg[:, h, :], blocks[:, :, C], 1.0, None, ALU.max).then_inc(T["deg"], 1)
                    dve.wait_ge(T["deg"], c + 1)
                    nc.vector.reciprocal(rdeg[:, h, :], deg[:, h, :]).then_inc(T["rdeg"], 1)
                    dve.wait_ge(T["rdeg"], c + 1)
                    nc.vector.tensor_tensor(cols(mean_msg), blocks[:, :, 0:C], wide(rdeg), ALU.mult).then_inc(T["mean"], 1)
                    dve.wait_ge(T["std"], c + 1)
                    nc.vector.reciprocal(nrstd[:, h, :], nstd[:, h, :]).then_inc(T["rstd"], 1)
                    dve.wait_ge(T["rstd"], c + 1)
                    dve.wait_ge(T["root"], c + 1)
                    if not first_is(c, 2):
                        dve.wait_ge(T["res"], c - 1)
                    nc.vector.tensor_tensor(cols(part), ps_root[h][:].rearrange("p (b c) -> p b c", c=C), wide(nrstd),
                                            ALU.mult).then_inc(T["part"], 1)
                    dve.wait_ge(T["mean"], c + 1)
                    dve.wait_ge(T["xb"], c + 1)
                    nc.vector.tensor_tensor(part2[:, h, :], mean_msg[:, h, :], xb[:, h, :], ALU.add).then_inc(T["part2"], 1)
                    dve.wait_ge(T["part2"], c + 1)
                    dve.wait_ge(T["part"], c + 1)

                def step(c, turn, slot):
                    h = slot % 2
                    combine(c, h)
                    if not first_is(c, 2):
                        dve.wait_ge(stored[h], turn * 32 + 16 * (slot // 2))
                    nc.vector.tensor_tensor(res[:, h, :], part[:, h, :], part2[:, h, :], ALU.add).then_inc(T["res"], 1)
                run_chunks(dve, step)


_INS = ['x', 'src', 'dst', 'edge_attr_2', 'L0_gnn_weight', 'L0_gnn_root_w', 'L0_gnn_root_b']
_OUTS = [((100000, 32), 'float32')]


def kernel(**inputs):
    import numpy as _np
    import concourse.bacc as _bacc
    from concourse import mybir as _mybir
    from concourse.bass_utils import run_bass_kernel_spmd as _run

    nc = _bacc.Bacc("TRN2", target_bir_lowering=False, num_devices=1)
    arrays, args = {}, []
    for name in _INS:
        a = _np.ascontiguousarray(inputs[name])
        arrays[f"in_{name}_dram"] = a
        args.append(nc.dram_tensor(f"in_{name}_dram", a.shape, _mybir.dt.from_np(a.dtype), kind="ExternalInput").ap())
    for i, (shape, dtype) in enumerate(_OUTS):
        dt = _mybir.dt.from_np(_np.dtype(dtype))
        args.append(nc.dram_tensor(f"out_{i}_dram", shape, dt, kind="ExternalOutput").ap())
    build_gnn(nc, *args)
    r = _run(nc, [arrays], core_ids=[0])
    return r.results[0]["out_0_dram"]
```

```python
from collections import namedtuple
from contextlib import ExitStack

import concourse.bass as bass
from concourse import mybir

F32 = mybir.dt.float32
I32 = mybir.dt.int32
ALU = mybir.AluOpType
ACT = mybir.ActivationFunctionType
AX_X = mybir.AxisListType.X
ds = bass.ds

P = 128
GT = 4
SLOTS = 4
PLACE_LAG = 3
ADD_LAG = 4
HEAD = 6
LOOPS = ((6, 2), (8, 3), (7, 4))
BETWEEN = 4
PAD_NODE = 1 << 20
EPS = 1e-5
TABLE_STEPS = 6
RECIP_SHIFT = 9

Step = namedtuple("Step", "g turn slot place_win add_win")


def build_gnn(nc, x, src, dst, edge_attr, weight, root_w, root_b, out):
    N, C = x.shape
    E = src.shape[0]
    K = weight.shape[0]
    KS = 3
    D = edge_attr.shape[1]
    assert C == 32 and K == KS * KS and D == 2
    CW = C + 1
    J = 2
    SB = P * J
    NSB = -(-N // SB)
    BW = J * CW
    GRP = -(-(-(-E // P)) // GT)
    TILES = GRP * GT
    RC = 4
    RT = TILES // RC
    full_tiles, tail_edges = divmod(E, P)
    assert TILES == RC * RT and full_tiles - (RC - 1) * RT == 96
    assert HEAD + 4 * sum(n for n, _ in LOOPS) + BETWEEN * (len(LOOPS) - 1) == GRP

    SECTIONS, step_at = [], HEAD
    for n, (its, win) in enumerate(LOOPS):
        first_group = step_at - ADD_LAG if n else 0
        step_at += 4 * its + BETWEEN
        SECTIONS.append((first_group, GRP if n == len(LOOPS) - 1 else step_at - ADD_LAG, win))
    MAX_WIN = max(win for _, _, win in SECTIONS)
    WB = MAX_WIN * J
    for _, _, win in SECTIONS:
        assert all(n // win == n * -(-(1 << RECIP_SHIFT) // win) >> RECIP_SHIFT for n in range(NSB))

    CS = 8
    CB = CS * J
    CC = CB * C
    NCH = -(-NSB // CS)
    AGG_SB = max(NSB + MAX_WIN - 1, NCH * CS)
    XBUF = 4
    full_sb, tail_nodes = divmod(N, SB)
    tail_sb = full_sb - (NCH - 1) * CS
    QUADS = CB // 4

    with ExitStack() as ctx:
        def sb(name, shape, dt=F32):
            return ctx.enter_context(nc.sbuf_tensor(name, shape, dt))

        def sem(name):
            return ctx.enter_context(nc.semaphore(name))

        bank = [ctx.enter_context(nc.psum_tensor(f"bank{i}", [P, 512], F32)) for i in range(8)]

        agg = sb("agg", [P, AGG_SB * BW])
        ident = sb("ident", [P, P])
        iota_i = sb("iota_i", [P, P], I32)
        iota_row = sb("iota_row", [P, P])
        col_i = sb("col_i", [P, 1], I32)
        col_f = sb("col_f", [P, 1])
        eps = sb("eps", [P, 1])
        minus_grid = sb("minus_grid", [P, KS])
        zero = sb("zero", [P, 1])
        src_idx = sb("src_idx", [P, TILES], I32)
        minus_plane = sb("minus_plane", [P, TILES])
        rel = sb("rel", [P, TILES])
        attr = sb("attr", [P, D, TILES])
        basis = sb("basis", [P, K, TILES])
        mask = sb("mask", [P, TILES, WB])
        base_row = sb("base_row", [1, TILES], I32)
        sweeps_i = sb("sweeps_i", [1, 1], I32)
        w_bd = sb("w_bd", [P, K, P])
        root_bd = sb("root_bd", [P, P])
        root_t = sb("root_t", [P, P])
        center = sb("center", [P, P])
        quarter = sb("quarter", [P, 4])
        bias = sb("bias", [P, C])
        xin = sb("xin", [P, XBUF, CC])

        consts_made = sem("consts_made")
        pool_consts = sem("pool_consts")
        rows_padded = sem("rows_padded")
        rows_in = sem("rows_in")
        weights_in = sem("weights_in")
        root_in = sem("root_in")
        step_done = sem("step_done")
        agg_zero = sem("agg_zero")
        tables_up = sem("tables_up")
        range_up = sem("range_up")
        root_up = sem("root_up")
        x_in = [sem(f"x_in{s}") for s in range(XBUF)]

        CONSTS = 4 + 1 + 1 + KS + 8 + 2 + 1

        def chunk_view(a):
            return a[0:full_sb * SB, :].rearrange("(s p j) c -> p s (j c)", p=P, j=J)

        with ExitStack() as st:
            def tmp(name, shape, dt=F32):
                return st.enter_context(nc.sbuf_tensor(name, shape, dt))
            src_r = tmp("src_r", [RT, RC, P], I32)
            dst_r = tmp("dst_r", [RT, RC, P], I32)
            attr_r = tmp("attr_r", [RT, RC, P * D])
            src_f = tmp("src_f", [RT, RC, P])
            sb_i = tmp("sb_i", [RT, RC, P], I32)
            pl_i = tmp("pl_i", [RT, RC, P], I32)
            j_i = tmp("j_i", [RT, RC, P], I32)
            sb_f = tmp("sb_f", [RT, RC, P])
            sb_m = tmp("sb_m", [RT, RC, P])
            pl_f = tmp("pl_f", [RT, RC, P])
            j_f = tmp("j_f", [RT, RC, P])
            blk_f = tmp("blk_f", [RT, RC, P])
            rel_f = tmp("rel_f", [RT, RC, P])
            low = tmp("low", [RT, RC])
            low_c = tmp("low_c", [RT, RC])
            high = tmp("high", [RT, RC])
            span = tmp("span", [RT, RC])
            span_w = tmp("span_w", [1, len(SECTIONS)])
            span_i = tmp("span_i", [1, len(SECTIONS)], I32)
            span_s = tmp("span_s", [1, len(SECTIONS)], I32)
            widest = tmp("widest", [1, 1])
            block = st.enter_context(nc.Block())

            def dram_rows(a, width):
                n = (RC - 1) * RT * P
                if width == 1:
                    return (a[0:n].rearrange("(c r p) -> r c p", r=RT, p=P),
                            a[n:full_tiles * P].rearrange("(r p) -> r p", p=P),
                            a[full_tiles * P:E].rearrange("(r p) -> r p", r=1))
                return (a[0:n, :].rearrange("(c r p) d -> r c (p d)", r=RT, p=P),
                        a[n:full_tiles * P, :].rearrange("(r p) d -> r (p d)", p=P),
                        a[full_tiles * P:E, :].rearrange("(r p) d -> r (p d)", r=1))

            def load_table(eng, table, a, width):
                most, rest, last = dram_rows(a, width)
                eng.dma_start(table[:, 0:RC - 1, :], most).then_inc(rows_in, 16)
                eng.dma_start(table[0:96, RC - 1, :], rest).then_inc(rows_in, 16)
                eng.dma_start(table[96:97, RC - 1, 0:tail_edges * width], last).then_inc(rows_in, 16)

            @block.sync
            def _(sp):
                sp.wait_ge(rows_padded, 3)
                load_table(sp, dst_r, dst, 1)
                load_table(sp, src_r, src, 1)
                sp.wait_ge(consts_made, 5)
                for b in range(4):
                    rows = slice(b * C, (b + 1) * C)
                    sp.dma_start(w_bd[rows, :, rows], weight.rearrange("k i o -> i k o")).then_inc(weights_in, 16)
                for c in range(XBUF):
                    sp.dma_start(xin[:, c, :].rearrange("p (s e) -> p s e", s=CS),
                                 chunk_view(x)[:, c * CS:(c + 1) * CS, :]).then_inc(x_in[c], 16)

            @block.scalar
            def _(act):
                act.wait_ge(rows_padded, 3)
                load_table(act, attr_r, edge_attr, D)
                act.wait_ge(consts_made, 5)
                for b in range(4):
                    act.dma_start(root_bd[b * C:(b + 1) * C, b * C:(b + 1) * C], root_w).then_inc(root_in, 16)
                act.dma_start(bias[:], root_b.rearrange("(a c) -> a c", a=1).broadcast_to([P, C])).then_inc(root_in, 16)
                act.wait_ge(consts_made, 6)
                half = agg.shape[1] // 2
                nc.scalar.copy(agg[:, 0:half], zero[:].broadcast_to([P, half])).then_inc(agg_zero, 1)

            @block.gpsimd
            def _(pool):
                nc.gpsimd.iota(iota_i[:], pattern=[[1, P]], base=0, channel_multiplier=0).then_inc(pool_consts, 1)
                nc.gpsimd.iota(col_i[:], pattern=[[1, 1]], base=0, channel_multiplier=1).then_inc(pool_consts, 1)
                nc.gpsimd.memset(agg[:, agg.shape[1] // 2:], 0.0).then_inc(agg_zero, 1)

            @block.vector
            def _(dve):
                done = [0]

                def step(ins):
                    done[0] += 1
                    ins.then_inc(step_done, 1)
                    dve.wait_ge(step_done, done[0])

                for table, fill in ((dst_r, PAD_NODE), (src_r, 0), (attr_r, 0)):
                    nc.vector.memset(table[96:RT, RC - 1, :], fill).then_inc(rows_padded, 1)
                for cleared in (w_bd, root_bd, center, quarter):
                    nc.vector.memset(cleared[:], 0.0).then_inc(consts_made, 1)
                nc.vector.memset(eps[:], EPS).then_inc(consts_made, 1)
                nc.vector.memset(zero[:], 0.0).then_inc(consts_made, 1)
                for a in range(KS):
                    nc.vector.memset(minus_grid[:, a:a + 1], -a / (KS - 1)).then_inc(consts_made, 1)
                dve.wait_ge(consts_made, 6)
                for b in range(4):
                    rows = slice(b * C, (b + 1) * C)
                    nc.vector.memset(center[rows, rows], -1.0 / C).then_inc(consts_made, 1)
                    nc.vector.memset(quarter[rows, b:b + 1], 1.0 / C).then_inc(consts_made, 1)
                dve.wait_ge(pool_consts, 2)
                nc.vector.tensor_copy(iota_row[:], iota_i[:]).then_inc(consts_made, 1)
                nc.vector.tensor_copy(col_f[:], col_i[:]).then_inc(consts_made, 1)
                dve.wait_ge(consts_made, CONSTS - 1)
                nc.vector.tensor_scalar(ident[:], iota_row[:], col_f[:, 0:1], None, ALU.is_equal).then_inc(consts_made, 1)
                dve.wait_ge(consts_made, CONSTS)
                step(nc.vector.tensor_tensor(center[:], center[:], ident[:], ALU.add))
                dve.wait_ge(rows_in, 9 * 16)
                nc.vector.tensor_scalar(sb_i[:], dst_r[:], 8, None, ALU.logical_shift_right)
                nc.vector.tensor_scalar(j_i[:], dst_r[:], 1, None, ALU.bitwise_and)
                step(nc.vector.tensor_scalar(pl_i[:], dst_r[:], 1, P - 1, ALU.logical_shift_right, ALU.bitwise_and))
                nc.vector.tensor_copy(sb_f[:], sb_i[:])
                nc.vector.tensor_copy(src_f[:], src_r[:])
                nc.vector.tensor_copy(pl_f[:], pl_i[:])
                step(nc.vector.tensor_copy(j_f[:], j_i[:]))
                nc.vector.tensor_reduce(low[:], sb_f[:], AX_X, ALU.min)
                nc.vector.scalar_tensor_tensor(out=sb_m[:], in0=sb_f[:], scalar=float(PAD_NODE // SB), in1=sb_f[:],
                                               op0=ALU.is_lt, op1=ALU.mult)
                step(nc.vector.scalar_tensor_tensor(out=blk_f[:], in0=sb_f[:], scalar=float(J), in1=j_f[:],
                                                    op0=ALU.mult, op1=ALU.add))
                nc.vector.tensor_reduce(high[:], sb_m[:], AX_X, ALU.max)
                step(nc.vector.tensor_scalar(low_c[:], low[:], float(NSB - 1), None, ALU.min))
                nc.vector.scalar_tensor_tensor(out=rel_f[:], in0=low_c[:].unsqueeze(2).broadcast_to([RT, RC, P]),
                                               scalar=-float(J), in1=blk_f[:], op0=ALU.mult, op1=ALU.add)
                step(nc.vector.tensor_tensor(span[:], high[:], low_c[:], ALU.subtract))
                assert done[0] == TABLE_STEPS
                dve.wait_ge(range_up, 1)
                nc.vector.tensor_copy(base_row[:], bank[5][0:1, 0:TILES])
                for n, (g0, g1, win) in enumerate(SECTIONS):
                    step(nc.vector.tensor_reduce(span_w[:, n:n + 1], bank[4][0:1, g0 * GT:g1 * GT], AX_X, ALU.max))
                    step(nc.vector.tensor_scalar(span_i[:, n:n + 1], span_w[:, n:n + 1],
                                                 float(-(-(1 << RECIP_SHIFT) // win)), None, ALU.mult))
                step(nc.vector.tensor_scalar(span_s[:], span_i[:], RECIP_SHIFT, None, ALU.arith_shift_right))
                step(nc.vector.tensor_reduce(widest[:], span_s[:], AX_X, ALU.max))
                step(nc.vector.tensor_scalar(sweeps_i[:], widest[:], 1.0, None, ALU.add))
                dve.wait_ge(tables_up, 5)
                nc.vector.tensor_copy(src_idx[:], bank[0][:, 0:TILES])
                nc.vector.tensor_scalar(minus_plane[:], bank[1][:, 0:TILES], -1.0, None, ALU.mult)
                nc.vector.tensor_copy(rel[:], bank[2][:, 0:TILES])
                for d in range(D):
                    nc.vector.tensor_scalar(attr[:, d, :], bank[(6, 7)[d]][:, 0:TILES], 0.0, 1.0, ALU.max, ALU.min)
                dve.wait_ge(root_up, 1)
                step(nc.vector.tensor_copy(root_t[:], bank[3][:, 0:P]))
                dve.wait_ge(agg_zero, 2)

            @block.tensor
            def _(pe):
                pe.wait_ge(consts_made, CONSTS)
                pe.wait_ge(root_in, 80)
                nc.tensor.transpose(bank[3][:, 0:P], root_bd[:], ident[:]).then_inc(root_up, 1)
                pe.wait_ge(rows_in, 9 * 16)
                for d in range(D):
                    for c in range(RC):
                        last = nc.tensor.transpose(bank[(6, 7)[d]][:, c * RT:(c + 1) * RT],
                                                   attr_r[:, c, :].rearrange("r (p d) -> r p d", d=D)[:, :, d],
                                                   ident[0:RT, 0:RT])
                    last.then_inc(tables_up, 1)
                pe.wait_ge(step_done, TABLE_STEPS)
                for i, row in ((5, low_c), (4, span)):
                    for c in range(RC):
                        last = nc.tensor.transpose(bank[i][0:1, c * RT:(c + 1) * RT], row[:, c:c + 1], ident[0:RT, 0:RT])
                last.then_inc(range_up, 1)
                for i, table in enumerate((src_f, pl_f, rel_f)):
                    for c in range(RC):
                        last = nc.tensor.transpose(bank[i][:, c * RT:(c + 1) * RT], table[:, c, :], ident[0:RT, 0:RT])
                    last.then_inc(tables_up, 1)

        with ExitStack() as st:
            def tmp(name, shape, dt=F32):
                return st.enter_context(nc.sbuf_tensor(name, shape, dt))
            idx_slot = [tmp(f"idx_slot{s}", [P, GT], I32) for s in range(SLOTS)]
            xg = [tmp(f"xg{s}", [P, GT, C]) for s in range(SLOTS)]
            dist = tmp("dist", [P, D, TILES])
            hat = tmp("hat", [P, KS, D, TILES])
            xc = tmp("xc", [P, GT, C])
            xr = tmp("xr", [P, GT, C])
            sq = tmp("sq", [P, GT, C])
            row_sum = tmp("row_sum", [P, GT])
            sq_sum = tmp("sq_sum", [P, GT])
            std = tmp("std", [P, GT])
            rstd = tmp("rstd", [P, GT])
            scaled = tmp("scaled", [P, K, GT])
            spread = [tmp(f"spread{s}", [P, K, GT, C]) for s in range(2)]
            spread_t = [tmp(f"spread_t{s}", [P, K, P]) for s in range(2)]
            msg = [tmp(f"msg{s}", [P, GT, CW]) for s in range(2)]
            away = tmp("away", [P, GT, P])
            onehot = [tmp(f"onehot{s}", [P, GT, P]) for s in range(2)]
            placed = [tmp(f"placed{s}", [P, GT, WB, CW]) for s in range(2)]
            KB = 3
            ps_spread, ps_msg, ps_win = bank[0:3], bank[3], bank[4:8]

            S = {n: sem(n) for n in (
                "idx_ready", "dist_done", "hats_done", "mask_done", "basis_done", "ones_set", "sum_done", "xc_done",
                "sq_done", "relu_done", "sqsum_done", "std_done", "rstd_done", "scaled_done", "spread_done",
                "turned", "turned_out", "msg_made", "msg_out", "away_done", "onehot_done", "placed_done",
                "win_made", "win_added", "moved_on")}
            landed = [sem(f"landed{s}") for s in range(SLOTS)]
            sweep_sems = list(S.values()) + landed

            def win_of(g):
                return next(win for g0, g1, win in SECTIONS if g0 <= g < g1)

            def run_steps(eng, step, drain=True, spare=0):
                def by_hand(g0, g1):
                    for g in range(g0, g1):
                        step(Step(g, g // 4, g % 4, *(win_of(g - lag) if 0 <= g - lag < GRP else None
                                                      for lag in (PLACE_LAG, ADD_LAG))))
                by_hand(0, HEAD)
                at = HEAD
                for n, (its, win) in enumerate(LOOPS):
                    if n:
                        by_hand(at, at + BETWEEN)
                        at += BETWEEN
                    its -= spare if n == len(LOOPS) - 1 else 0
                    assert at % 4 == HEAD % 4
                    with eng.Fori(at // 4, at // 4 + its) as i:
                        for u in range(HEAD % 4, HEAD % 4 + 4):
                            step(Step(i * 4 + u, i + u // 4, u % 4, win, win))
                    at += 4 * its
                by_hand(at, GRP + ADD_LAG if drain else GRP)

            def is_group(g):
                return not isinstance(g, int) or 0 <= g < GRP

            def after(g, n):
                return not isinstance(g, int) or g >= n

            def tiles(g):
                return slice(g * GT, (g + 1) * GT) if isinstance(g, int) else ds(g * GT, GT)

            sweeps = nc.values_load(sweeps_i[0:1, 0:1], min_val=1, max_val=NSB)
            with nc.Fori(0, sweeps):
                with nc.Block() as block:
                    @block.gpsimd
                    def _(pool):
                        def step(s):
                            pool.wait_ge(S["idx_ready"], s.g + 1)
                            pool.nop(nofuse=True)
                            for t in range(GT):
                                nc.gpsimd.indirect_dma_start(
                                    out=xg[s.slot][:, t, :], out_offset=None, in_=x,
                                    in_offset=bass.IndirectOffsetOnAxis(idx_slot[s.slot][:, t:t + 1], 0),
                                ).then_inc(landed[s.slot], 16)
                        run_steps(pool, step, drain=False)

                    @block.scalar
                    def _(act):
                        def give_indices(g, slot):
                            nc.scalar.copy(idx_slot[slot][:], src_idx[:, tiles(g)]).then_inc(S["idx_ready"], 1)

                        def take_turned(g, h, banks):
                            for n in banks:
                                if n == 0 and after(g, 2):
                                    act.wait_ge(S["msg_made"], g - 1)
                                act.wait_ge(S["turned"], g * (K // KB) + (n + 1))
                                nc.scalar.copy(spread_t[h][:, n * KB:(n + 1) * KB, :],
                                               ps_spread[n][:, 0:KB * P].rearrange("p (k e) -> p k e", k=KB)
                                               ).then_inc(S["turned_out"], 1)

                        def square_relu(g):
                            act.wait_ge(S["xc_done"], g + 1)
                            nc.scalar.activation(sq[:], xc[:], ACT.Square).then_inc(S["sq_done"], 1)
                            nc.scalar.activation(xr[:], xc[:], ACT.Relu).then_inc(S["relu_done"], 1)

                        def deviation(g):
                            act.wait_ge(S["sqsum_done"], g + 1)
                            nc.scalar.activation(std[:], sq_sum[:], ACT.Sqrt, bias=eps[:, 0:1],
                                                 scale=1.0 / C).then_inc(S["std_done"], 1)

                        def one_hot(g, h):
                            if after(g, 1):
                                act.wait_ge(S["onehot_done"], g)
                            for t in range(GT):
                                at = g * GT + t
                                b = minus_plane[:, at:at + 1] if isinstance(g, int) else minus_plane[:, ds(at, 1)]
                                nc.scalar.activation(away[:, t, :], iota_row[:], ACT.Square, bias=b
                                                     ).then_inc(S["away_done"], 1)
                            if after(g, 2):
                                act.wait_ge(S["win_made"], (g - 1) * GT)
                            act.wait_ge(S["away_done"], (g + 1) * GT)
                            nc.scalar.activation(onehot[h][:], away[:], ACT.Relu, bias=1.0, scale=-1.0
                                                 ).then_inc(S["onehot_done"], 1)

                        def take_messages(g, h):
                            if after(g, 2):
                                act.wait_ge(S["placed_done"], g - 1)
                            act.wait_ge(S["msg_made"], g + 1)
                            nc.scalar.copy(msg[h][:, :, 0:C], ps_msg[:, 0:GT * C].rearrange("p (t c) -> p t c", t=GT)
                                           ).then_inc(S["msg_out"], 1)

                        def step(s):
                            turned = after(s.g, 1) and is_group(s.g - 1)
                            if is_group(s.g):
                                square_relu(s.g)
                                if is_group(s.g + SLOTS):
                                    give_indices(s.g + SLOTS, s.slot)
                            if turned:
                                take_turned(s.g - 1, (s.slot - 1) % 2, [0])
                            if is_group(s.g):
                                deviation(s.g)
                            if turned:
                                take_turned(s.g - 1, (s.slot - 1) % 2, range(1, K // KB))
                            if after(s.g, 2) and is_group(s.g - 2):
                                take_messages(s.g - 2, s.slot % 2)
                                one_hot(s.g - 2, s.slot % 2)

                        for g in range(SLOTS):
                            give_indices(g, g)
                        for a in range(KS):
                            if a:
                                act.wait_ge(S["hats_done"], a)
                            nc.scalar.activation(dist[:], attr[:], ACT.Abs, bias=minus_grid[:, a:a + 1]
                                                 ).then_inc(S["dist_done"], 1)
                            act.wait_ge(S["dist_done"], a + 1)
                            nc.scalar.activation(hat[:, a, :, :], dist[:], ACT.Relu, bias=1.0, scale=-float(KS - 1)
                                                 ).then_inc(S["hats_done"], 1)
                        run_steps(act, step, spare=1)

                    @block.vector
                    def _(dve):
                        for h in range(2):
                            nc.vector.memset(msg[h][:, :, C:CW], 1.0).then_inc(S["ones_set"], 1)
                        nc.vector.tensor_tensor(
                            mask[:], rel[:].unsqueeze(2).broadcast_to([P, TILES, WB]),
                            iota_row[:, 0:WB].unsqueeze(1).broadcast_to([P, TILES, WB]),
                            ALU.is_equal).then_inc(S["mask_done"], 1)
                        dve.wait_ge(S["hats_done"], KS)
                        for k in range(K):
                            nc.vector.tensor_tensor(basis[:, k, :], hat[:, k // KS, 0, :], hat[:, k % KS, 1, :],
                                                    ALU.mult).then_inc(S["basis_done"], 1)
                        dve.wait_ge(S["basis_done"], K)
                        dve.wait_ge(S["mask_done"], 1)
                        dve.wait_ge(S["ones_set"], 2)

                        def sum_rows(g, turn, slot):
                            dve.wait_ge(landed[slot], turn * (16 * GT) + 16 * GT)
                            nc.vector.tensor_reduce(row_sum[:], xg[slot][:], AX_X, ALU.add).then_inc(S["sum_done"], 1)

                        def center_rows(g, slot):
                            dve.wait_ge(S["sum_done"], g + 1)
                            nc.vector.scalar_tensor_tensor(
                                out=xc[:], in0=row_sum[:].unsqueeze(2).broadcast_to([P, GT, C]),
                                scalar=-1.0 / C, in1=xg[slot][:], op0=ALU.mult, op1=ALU.add).then_inc(S["xc_done"], 1)

                        def place(g, h, win):
                            if after(g, 2):
                                dve.wait_ge(S["win_made"], (g - 1) * GT)
                            dve.wait_ge(S["msg_out"], g + 1)
                            shape = [P, GT, win * J, CW]
                            nc.vector.tensor_tensor(
                                placed[h][:, :, 0:win * J, :],
                                mask[:, tiles(g), 0:win * J].unsqueeze(3).broadcast_to(shape),
                                msg[h][:].unsqueeze(2).broadcast_to(shape), ALU.mult).then_inc(S["placed_done"], 1)

                        def sum_squares(g):
                            dve.wait_ge(S["sq_done"], g + 1)
                            nc.vector.tensor_reduce(sq_sum[:], sq[:], AX_X, ALU.add).then_inc(S["sqsum_done"], 1)

                        def invert_deviation(g):
                            dve.wait_ge(S["std_done"], g + 1)
                            nc.vector.reciprocal(rstd[:], std[:]).then_inc(S["rstd_done"], 1)

                        def scale_basis(g):
                            dve.wait_ge(S["rstd_done"], g + 1)
                            nc.vector.tensor_tensor(scaled[:], basis[:, :, tiles(g)],
                                                    rstd[:].unsqueeze(1).broadcast_to([P, K, GT]),
                                                    ALU.mult).then_inc(S["scaled_done"], 1)

                        def spread_rows(g, h):
                            dve.wait_ge(S["scaled_done"], g + 1)
                            shape = [P, K, GT, C]
                            nc.vector.tensor_tensor(spread[h][:], xr[:].unsqueeze(1).broadcast_to(shape),
                                                    scaled[:].unsqueeze(3).broadcast_to(shape), ALU.mult
                                                    ).then_inc(S["spread_done"], 1)

                        def window_starts(g):
                            _, values = nc.values_load_multi_w_load_instructions(
                                base_row[0:1, tiles(g)], engines=[dve.engine], min_val=0, max_val=NSB - 1,
                                skip_runtime_bounds_check_because="made below NSB")
                            return values

                        def add_window(g, t, win, start):
                            if after(g * GT + t, 1):
                                dve.wait_ge(S["win_added"], g * GT + t)
                            a = agg[:, ds(start * BW, win * BW)]
                            nc.vector.tensor_tensor(a, a, ps_win[t][:, 0:win * BW], ALU.add
                                                    ).then_inc(S["win_added"], 1)

                        def step(s):
                            now, add = is_group(s.g), after(s.g, ADD_LAG)
                            if now:
                                if after(s.g, 2):
                                    dve.wait_ge(S["turned"], (s.g - 1) * (K // KB))
                                sum_rows(s.g, s.turn, s.slot)
                            if after(s.g, PLACE_LAG) and is_group(s.g - PLACE_LAG):
                                place(s.g - PLACE_LAG, (s.slot - PLACE_LAG) % 2, s.place_win)
                            if add:
                                old = s.g - ADD_LAG
                                starts = window_starts(old)
                            if now:
                                center_rows(s.g, s.slot)
                            if add:
                                dve.wait_ge(S["win_made"], (old + 1) * GT)
                                add_window(old, 0, s.add_win, starts[0])
                            if now:
                                sum_squares(s.g)
                            if add:
                                add_window(old, 1, s.add_win, starts[1])
                            if now:
                                invert_deviation(s.g)
                            if add:
                                add_window(old, 2, s.add_win, starts[2])
                            if now:
                                scale_basis(s.g)
                            if add:
                                add_window(old, 3, s.add_win, starts[3])
                            if now:
                                spread_rows(s.g, s.slot % 2)
                        run_steps(dve, step)
                        dve.wait_ge(S["win_added"], TILES)
                        for g0, g1, win in SECTIONS:
                            cols = slice(g0 * GT, g1 * GT)
                            nc.vector.tensor_scalar(rel[:, cols], rel[:, cols], -float(win * J), None, ALU.add
                                                    ).then_inc(S["moved_on"], 1)
                            nc.vector.tensor_scalar(base_row[:, cols], base_row[:, cols], float(win), float(NSB - 1),
                                                    ALU.add, ALU.min).then_inc(S["moved_on"], 1)
                        dve.wait_ge(S["moved_on"], 2 * len(SECTIONS))

                    @block.tensor
                    def _(pe):
                        def turn_spread(g, h):
                            if after(g, 1):
                                pe.wait_ge(S["turned_out"], g * (K // KB))
                            pe.wait_ge(S["spread_done"], g + 1)
                            for k in range(K):
                                last = nc.tensor.transpose(ps_spread[k // KB][:, k % KB * P:(k % KB + 1) * P],
                                                           spread[h][:, k, :, :].rearrange("p t c -> p (t c)"), ident[:])
                                if k % KB == KB - 1:
                                    last.then_inc(S["turned"], 1)

                        def make_messages(g, h):
                            if after(g, 1):
                                pe.wait_ge(S["msg_out"], g)
                            pe.wait_ge(S["turned_out"], (g + 1) * (K // KB))
                            for k in range(K):
                                last = nc.tensor.matmul(ps_msg[:, 0:GT * C], spread_t[h][:, k, :], w_bd[:, k, :],
                                                        start=(k == 0), stop=(k == K - 1))
                            last.then_inc(S["msg_made"], 1)

                        def make_windows(g, h, win):
                            pe.wait_ge(S["onehot_done"], g + 1)
                            pe.wait_ge(S["placed_done"], g + 1)
                            for t in range(GT):
                                if after(g, 1):
                                    pe.wait_ge(S["win_added"], (g - 1) * GT + (t + 1))
                                nc.tensor.matmul(ps_win[t][:, 0:win * BW], onehot[h][:, t, :],
                                                 placed[h][:, t, 0:win * J, :].rearrange("p w c -> p (w c)"),
                                                 start=True, stop=True).then_inc(S["win_made"], 1)

                        def step(s):
                            if after(s.g, 2) and is_group(s.g - 2):
                                make_messages(s.g - 2, s.slot % 2)
                            if after(s.g, PLACE_LAG) and is_group(s.g - PLACE_LAG):
                                make_windows(s.g - PLACE_LAG, (s.slot - PLACE_LAG) % 2, s.place_win)
                            if is_group(s.g):
                                turn_spread(s.g, s.slot % 2)

                        pe.wait_ge(weights_in, 64)
                        run_steps(pe, step)

                nums = sorted(s.num for s in sweep_sems)
                assert nums == list(range(nums[0], nums[0] + len(nums)))
                nc.gpsimd.dma_reset(range(nums[0], nums[-1] + 1))
                nc.gpsimd.sem_clear(range(nums[0], nums[-1] + 1))
                nc.all_engine_barrier()

        with ExitStack() as st:
            def tmp(name, shape, dt=F32):
                return st.enter_context(nc.sbuf_tensor(name, shape, dt))
            xb = tmp("xb", [P, 2, CC])
            x_t = tmp("x_t", [P, 2, CC])
            relu_t = tmp("relu_t", [P, 2, CC])
            sq_t = tmp("sq_t", [P, 2, CC])
            nstd = tmp("nstd", [P, 2, CB])
            nrstd = tmp("nrstd", [P, 2, CB])
            deg = tmp("deg", [P, NCH * CB])
            rdeg = tmp("rdeg", [P, NCH * CB])
            mean_msg = tmp("mean_msg", [P, 2, CC])
            part = tmp("part", [P, 2, CC])
            part2 = tmp("part2", [P, 2, CC])
            res = tmp("res", [P, 2, CC])
            ps_xt, ps_xc, ps_root, ps_var = bank[0:2], bank[2:4], bank[4:6], bank[6:8]
            stored = [sem(f"stored{s}") for s in range(2)]
            T = {n: sem("n_" + n) for n in (
                "xt", "xt_out", "xc", "relu", "sq", "var", "root", "std", "rstd", "xb", "deg", "rdeg",
                "mean", "part", "part2", "res")}
            assert (NCH - 9) % 4 == 0
            NL = (NCH - 9) // 4

            def tail_view(a):
                return a[full_sb * SB:N, :].rearrange("(p j) c -> p (j c)", j=J)

            block = st.enter_context(nc.Block())

            def run_chunks(eng, step):
                for c in range(4):
                    step(c, 0, c)
                with eng.Fori(0, NL) as i:
                    for u in range(4):
                        step(i * 4 + (4 + u), i + 1, u)
                for c in range(NCH - 5, NCH):
                    step(c, c // 4, c % 4)

            def cut(a, c, n):
                return a[:, c * n:(c + 1) * n] if isinstance(c, int) else a[:, ds(c * n, n)]

            def first_is(c, n):
                return isinstance(c, int) and c < n

            @block.sync
            def _(sp):
                views, out_views = chunk_view(x), chunk_view(out)
                LAST = NCH - 1

                def rows(view, c):
                    return view[:, c * CS:(c + 1) * CS, :] if isinstance(c, int) else view[:, ds(c * CS, CS), :]

                def load(c, slot):
                    sp.wait_ge(T["xt"], c - (XBUF - 1))
                    sp.wait_ge(T["xb"], c - (XBUF - 1))
                    if isinstance(c, int) and c == LAST:
                        sp.dma_start(xin[:, slot, 0:tail_sb * J * C].rearrange("p (s e) -> p s e", s=tail_sb),
                                     views[:, c * CS:c * CS + tail_sb, :]).then_inc(x_in[slot], 16)
                        sp.dma_start(xin[0:tail_nodes // J, slot, tail_sb * J * C:(tail_sb + 1) * J * C],
                                     tail_view(x)).then_inc(x_in[slot], 16)
                    else:
                        sp.dma_start(xin[:, slot, :].rearrange("p (s e) -> p s e", s=CS),
                                     rows(views, c)).then_inc(x_in[slot], 16)

                def store(c, h):
                    sp.wait_ge(T["res"], c + 1)
                    if isinstance(c, int) and c == LAST:
                        sp.dma_start(views_tail(out_views), res[:, h, 0:tail_sb * J * C].rearrange(
                            "p (s e) -> p s e", s=tail_sb)).then_inc(stored[h], 16)
                        sp.dma_start(tail_view(out), res[0:tail_nodes // J, h, tail_sb * J * C:(tail_sb + 1) * J * C]
                                     ).then_inc(stored[h], 16)
                    else:
                        sp.dma_start(rows(out_views, c), res[:, h, :].rearrange("p (s e) -> p s e", s=CS)
                                     ).then_inc(stored[h], 16)

                def views_tail(view):
                    return view[:, LAST * CS:LAST * CS + tail_sb, :]

                with sp.Fori(0, (NCH - 5) // 4) as i:
                    for u in range(4):
                        load(i * 4 + (4 + u), u)
                        store(i * 4 + u, u % 2)
                load(LAST, LAST % XBUF)
                for c in range(NCH - 5, NCH):
                    store(c, c % 2)
                sp.wait_ge(stored[0], 16 * (NCH // 2) + 32)
                sp.wait_ge(stored[1], 16 * (NCH // 2))

            def landed_count(c, turn):
                return turn * 16 + (32 if first_is(c, NCH) and c == NCH - 1 else 16)

            @block.gpsimd
            def _(pool):
                def step(c, turn, slot):
                    h = slot % 2
                    pool.wait_ge(x_in[slot], landed_count(c, turn))
                    nc.gpsimd.tensor_tensor(xb[:, h, :].rearrange("p (b c) -> p b c", c=C),
                                            xin[:, slot, :].rearrange("p (b c) -> p b c", c=C),
                                            bias[:].unsqueeze(1).broadcast_to([P, CB, C]), ALU.add).then_inc(T["xb"], 1)
                    pool.wait_ge(T["xb"], c + 1)
                    if not first_is(c, 2):
                        pool.wait_ge(T["res"], c - 1)
                    pool.wait_ge(T["mean"], c + 1)
                    nc.gpsimd.tensor_tensor(part2[:, h, :], mean_msg[:, h, :], xb[:, h, :], ALU.add).then_inc(T["part2"], 1)
                run_chunks(pool, step)

            @block.tensor
            def _(pe):
                def turn_in(c, turn, slot):
                    h = slot % 2
                    pe.wait_ge(x_in[slot], landed_count(c, turn))
                    if not first_is(c, 2):
                        pe.wait_ge(T["xt_out"], c - 1)
                    for q in range(QUADS):
                        last = nc.tensor.transpose(ps_xt[h][:, q * P:(q + 1) * P], xin[:, slot, q * P:(q + 1) * P], ident[:])
                    last.then_inc(T["xt"], 1)

                def centre(c, h):
                    if not first_is(c, 2):
                        pe.wait_ge(T["relu"], c - 1)
                    pe.wait_ge(T["xt_out"], c + 1)
                    nc.tensor.matmul(ps_xc[h][:], center[:], x_t[:, h, :], start=True, stop=True).then_inc(T["xc"], 1)

                def variance(c, h):
                    if not first_is(c, 2):
                        pe.wait_ge(T["std"], c - 1)
                    pe.wait_ge(T["sq"], c + 1)
                    for q in range(QUADS):
                        last = nc.tensor.matmul(ps_var[h][:, q * 4:(q + 1) * 4], sq_t[:, h, q * P:(q + 1) * P], quarter[:],
                                                start=True, stop=True)
                    last.then_inc(T["var"], 1)

                def root_product(c, h):
                    if not first_is(c, 2):
                        pe.wait_ge(T["part"], c - 1)
                    pe.wait_ge(T["relu"], c + 1)
                    for q in range(QUADS):
                        last = nc.tensor.matmul(ps_root[h][:, q * P:(q + 1) * P], relu_t[:, h, q * P:(q + 1) * P], root_t[:],
                                                start=True, stop=True)
                    last.then_inc(T["root"], 1)

                def step(c, turn, slot):
                    h = slot % 2
                    centre(c, h)
                    if not first_is(c, 1):
                        root_product(c - 1, 1 - h)
                    if not (isinstance(c, int) and c == NCH - 1):
                        turn_in(c + 1, turn + (slot + 1) // 4, (slot + 1) % 4)
                    variance(c, h)
                turn_in(0, 0, 0)
                run_chunks(pe, step)
                root_product(NCH - 1, (NCH - 1) % 2)

            @block.scalar
            def _(act):
                def copy_turned(c, h):
                    if not first_is(c, 2):
                        act.wait_ge(T["xc"], c - 1)
                    act.wait_ge(T["xt"], c + 1)
                    nc.scalar.copy(x_t[:, h, :], ps_xt[h][:]).then_inc(T["xt_out"], 1)

                def step(c, turn, slot):
                    h = slot % 2
                    if not first_is(c, 2):
                        act.wait_ge(T["root"], c - 1)
                        act.wait_ge(T["var"], c - 1)
                    act.wait_ge(T["xc"], c + 1)
                    nc.scalar.activation(sq_t[:, h, :], ps_xc[h][:], ACT.Square).then_inc(T["sq"], 1)
                    nc.scalar.activation(relu_t[:, h, :], ps_xc[h][:], ACT.Relu).then_inc(T["relu"], 1)
                    if not (isinstance(c, int) and c == NCH - 1):
                        copy_turned(c + 1, 1 - h)
                    if not first_is(c, 2):
                        act.wait_ge(T["rstd"], c - 1)
                    act.wait_ge(T["var"], c + 1)
                    nc.scalar.activation(nstd[:, h, :], ps_var[h][:, 0:CB], ACT.Sqrt, bias=eps[:, 0:1]).then_inc(T["std"], 1)
                copy_turned(0, 0)
                run_chunks(act, step)

            @block.vector
            def _(dve):
                agg_blocks = agg[:].rearrange("p (b e) -> p b e", e=CW)
                cols = lambda a, h: a[:, h, :].rearrange("p (b c) -> p b c", c=C)
                nc.vector.tensor_scalar(deg[:], agg_blocks[:, 0:NCH * CB, C], 1.0, None, ALU.max).then_inc(T["deg"], 1)
                dve.wait_ge(T["deg"], 1)
                nc.vector.reciprocal(rdeg[:], deg[:]).then_inc(T["rdeg"], 1)
                dve.wait_ge(T["rdeg"], 1)

                def mean_message(c, h):
                    if not first_is(c, 2):
                        dve.wait_ge(T["part2"], c - 1)
                    sums = agg_blocks[:, c * CB:(c + 1) * CB, 0:C] if isinstance(c, int) else (
                        cut(agg[:], c, CB * CW).rearrange("p (b e) -> p b e", e=CW)[:, :, 0:C])
                    nc.vector.tensor_tensor(cols(mean_msg, h), sums,
                                            cut(rdeg, c, CB).unsqueeze(2).broadcast_to([P, CB, C]),
                                            ALU.mult).then_inc(T["mean"], 1)

                def result(c, turn, slot, h):
                    if not first_is(c, 2):
                        dve.wait_ge(stored[h], turn * 32 + 16 * (slot // 2))
                    dve.wait_ge(T["part"], c + 1)
                    dve.wait_ge(T["part2"], c + 1)
                    nc.vector.tensor_tensor(res[:, h, :], part[:, h, :], part2[:, h, :], ALU.add).then_inc(T["res"], 1)

                def step(c, turn, slot):
                    h = slot % 2
                    mean_message(c, h)
                    if not first_is(c, 1):
                        result(c - 1, turn, slot - 1, 1 - h)
                    dve.wait_ge(T["std"], c + 1)
                    nc.vector.reciprocal(nrstd[:, h, :], nstd[:, h, :]).then_inc(T["rstd"], 1)
                    if not first_is(c, 2):
                        dve.wait_ge(T["res"], c - 1)
                    dve.wait_ge(T["rstd"], c + 1)
                    dve.wait_ge(T["root"], c + 1)
                    nc.vector.tensor_tensor(cols(part, h), ps_root[h][:].rearrange("p (b c) -> p b c", c=C),
                                            nrstd[:, h, :].unsqueeze(2).broadcast_to([P, CB, C]),
                                            ALU.mult).then_inc(T["part"], 1)
                run_chunks(dve, step)
                result(NCH - 1, (NCH - 1) // 4, (NCH - 1) % 4, (NCH - 1) % 2)


_INS = ['x', 'src', 'dst', 'edge_attr_2', 'L0_gnn_weight', 'L0_gnn_root_w', 'L0_gnn_root_b']
_OUTS = [((100000, 32), 'float32')]


def kernel(**inputs):
    import numpy as _np
    import concourse.bacc as _bacc
    from concourse import mybir as _mybir
    from concourse.bass_utils import run_bass_kernel_spmd as _run

    nc = _bacc.Bacc("TRN2", target_bir_lowering=False, num_devices=1)
    arrays, args = {}, []
    for name in _INS:
        a = _np.ascontiguousarray(inputs[name])
        arrays[f"in_{name}_dram"] = a
        args.append(nc.dram_tensor(f"in_{name}_dram", a.shape, _mybir.dt.from_np(a.dtype), kind="ExternalInput").ap())
    for i, (shape, dtype) in enumerate(_OUTS):
        dt = _mybir.dt.from_np(_np.dtype(dtype))
        args.append(nc.dram_tensor(f"out_{i}_dram", shape, dt, kind="ExternalOutput").ap())
    build_gnn(nc, *args)
    r = _run(nc, [arrays], core_ids=[0])
    return r.results[0]["out_0_dram"]
```

```python
from collections import namedtuple
from contextlib import ExitStack

import concourse.bass as bass
from concourse import mybir

F32 = mybir.dt.float32
I32 = mybir.dt.int32
ALU = mybir.AluOpType
ACT = mybir.ActivationFunctionType
AX_X = mybir.AxisListType.X
ds = bass.ds

P = 128
GT = 4
SLOTS = 4
PLACE_LAG = 4
ADD_LAG = 5
HEAD = 6
LOOPS = ((10, 2), (9, 3), (2, 4))
BETWEEN = 4
PAD_NODE = 1 << 20
EPS = 1e-5
TABLE_STEPS = 6
RECIP_SHIFT = 9

Step = namedtuple("Step", "g turn slot place_win add_win")


def build_gnn(nc, x, src, dst, edge_attr, weight, root_w, root_b, out):
    N, C = x.shape
    E = src.shape[0]
    K = weight.shape[0]
    KS = 3
    D = edge_attr.shape[1]
    assert C == 32 and K == KS * KS and D == 2
    CW = C + 1
    J = 2
    SB = P * J
    NSB = -(-N // SB)
    BW = J * CW
    GRP = -(-(-(-E // P)) // GT)
    TILES = GRP * GT
    RC = 4
    RT = TILES // RC
    full_tiles, tail_edges = divmod(E, P)
    assert TILES == RC * RT and full_tiles - (RC - 1) * RT == 96
    assert HEAD + 4 * sum(n for n, _ in LOOPS) + BETWEEN * (len(LOOPS) - 1) == GRP

    SECTIONS, step_at = [], HEAD
    for n, (its, win) in enumerate(LOOPS):
        first_group = step_at - ADD_LAG if n else 0
        step_at += 4 * its + BETWEEN
        SECTIONS.append((first_group, GRP if n == len(LOOPS) - 1 else step_at - ADD_LAG, win))
    MAX_WIN = max(win for _, _, win in SECTIONS)
    WB = MAX_WIN * J
    for _, _, win in SECTIONS:
        assert all(n // win == n * -(-(1 << RECIP_SHIFT) // win) >> RECIP_SHIFT for n in range(NSB))

    CS = 8
    CB = CS * J
    CC = CB * C
    NCH = -(-NSB // CS)
    AGG_SB = max(NSB + MAX_WIN - 1, NCH * CS)
    XBUF = 4
    full_sb, tail_nodes = divmod(N, SB)
    tail_sb = full_sb - (NCH - 1) * CS
    QUADS = CB // 4

    with ExitStack() as ctx:
        def sb(name, shape, dt=F32):
            return ctx.enter_context(nc.sbuf_tensor(name, shape, dt))

        def sem(name):
            return ctx.enter_context(nc.semaphore(name))

        bank = [ctx.enter_context(nc.psum_tensor(f"bank{i}", [P, 512], F32)) for i in range(8)]

        agg = sb("agg", [P, AGG_SB * BW])
        ident = sb("ident", [P, P])
        iota_i = sb("iota_i", [P, P], I32)
        iota_row = sb("iota_row", [P, P])
        col_i = sb("col_i", [P, 1], I32)
        col_f = sb("col_f", [P, 1])
        eps = sb("eps", [P, 1])
        minus_grid = sb("minus_grid", [P, KS])
        zero = sb("zero", [P, 1])
        src_idx = sb("src_idx", [P, TILES], I32)
        minus_plane = sb("minus_plane", [P, TILES])
        rel = sb("rel", [P, TILES])
        attr = sb("attr", [P, D, TILES])
        basis = sb("basis", [P, K, TILES])
        mask = sb("mask", [P, TILES, WB])
        base_row = sb("base_row", [1, TILES], I32)
        sweeps_i = sb("sweeps_i", [1, 1], I32)
        w_bd = sb("w_bd", [P, K, P])
        root_bd = sb("root_bd", [P, P])
        root_t = sb("root_t", [P, P])
        center = sb("center", [P, P])
        quarter = sb("quarter", [P, 4])
        bias = sb("bias", [P, C])
        xin = sb("xin", [P, XBUF, CC])

        consts_made = sem("consts_made")
        pool_consts = sem("pool_consts")
        rows_padded = sem("rows_padded")
        dst_in = sem("dst_in")
        src_in = sem("src_in")
        attr_in = sem("attr_in")
        src_floated = sem("src_floated")
        src_up = sem("src_up")
        src_idx_made = sem("src_idx_made")
        weights_in = sem("weights_in")
        root_in = sem("root_in")
        bias_in = sem("bias_in")
        step_done = sem("step_done")
        agg_zero = sem("agg_zero")
        attr_up = sem("attr_up")
        tables_up = sem("tables_up")
        range_up = sem("range_up")
        root_up = sem("root_up")
        x_in = [sem(f"x_in{s}") for s in range(XBUF)]

        CONSTS = 4 + 1 + 1 + KS + 8 + 2 + 1

        def chunk_view(a):
            return a[0:full_sb * SB, :].rearrange("(s p j) c -> p s (j c)", p=P, j=J)

        with ExitStack() as st:
            def tmp(name, shape, dt=F32):
                return st.enter_context(nc.sbuf_tensor(name, shape, dt))
            src_r = tmp("src_r", [RT, RC, P], I32)
            dst_r = tmp("dst_r", [RT, RC, P], I32)
            attr_r = tmp("attr_r", [RT, RC, P * D])
            src_f = tmp("src_f", [RT, RC, P])
            sb_i = tmp("sb_i", [RT, RC, P], I32)
            pl_i = tmp("pl_i", [RT, RC, P], I32)
            j_i = tmp("j_i", [RT, RC, P], I32)
            sb_f = tmp("sb_f", [RT, RC, P])
            sb_m = tmp("sb_m", [RT, RC, P])
            pl_f = tmp("pl_f", [RT, RC, P])
            j_f = tmp("j_f", [RT, RC, P])
            blk_f = tmp("blk_f", [RT, RC, P])
            rel_f = tmp("rel_f", [RT, RC, P])
            low = tmp("low", [RT, RC])
            low_c = tmp("low_c", [RT, RC])
            high = tmp("high", [RT, RC])
            span = tmp("span", [RT, RC])
            span_w = tmp("span_w", [1, len(SECTIONS)])
            span_i = tmp("span_i", [1, len(SECTIONS)], I32)
            span_s = tmp("span_s", [1, len(SECTIONS)], I32)
            widest = tmp("widest", [1, 1])
            ZERO_ACT = agg.shape[1] * 6 // 32
            block = st.enter_context(nc.Block())

            def dram_rows(a, width):
                n = (RC - 1) * RT * P
                if width == 1:
                    return (a[0:n].rearrange("(c r p) -> r c p", r=RT, p=P),
                            a[n:full_tiles * P].rearrange("(r p) -> r p", p=P),
                            a[full_tiles * P:E].rearrange("(r p) -> r p", r=1))
                return (a[0:n, :].rearrange("(c r p) d -> r c (p d)", r=RT, p=P),
                        a[n:full_tiles * P, :].rearrange("(r p) d -> r (p d)", p=P),
                        a[full_tiles * P:E, :].rearrange("(r p) d -> r (p d)", r=1))

            def load_table(eng, table, a, width, rows_in):
                most, rest, last = dram_rows(a, width)
                eng.dma_start(table[:, 0:RC - 1, :], most).then_inc(rows_in, 16)
                eng.dma_start(table[0:96, RC - 1, :], rest).then_inc(rows_in, 16)
                eng.dma_start(table[96:97, RC - 1, 0:tail_edges * width], last).then_inc(rows_in, 16)

            @block.sync
            def _(sp):
                sp.wait_ge(rows_padded, 1)
                load_table(sp, dst_r, dst, 1, dst_in)
                sp.wait_ge(rows_padded, 2)
                load_table(sp, src_r, src, 1, src_in)
                sp.wait_ge(consts_made, 3)
                for b in range(4):
                    sp.dma_start(root_bd[b * C:(b + 1) * C, b * C:(b + 1) * C], root_w).then_inc(root_in, 16)
                for b in range(4):
                    rows = slice(b * C, (b + 1) * C)
                    sp.dma_start(w_bd[rows, :, rows], weight.rearrange("k i o -> i k o")).then_inc(weights_in, 16)
                for c in range(XBUF):
                    sp.dma_start(xin[:, c, :].rearrange("p (s e) -> p s e", s=CS),
                                 chunk_view(x)[:, c * CS:(c + 1) * CS, :]).then_inc(x_in[c], 16)

            @block.scalar
            def _(act):
                act.wait_ge(rows_padded, 3)
                load_table(act, attr_r, edge_attr, D, attr_in)
                act.dma_start(bias[:], root_b.rearrange("(a c) -> a c", a=1).broadcast_to([P, C])).then_inc(bias_in, 16)
                act.wait_ge(consts_made, 1)
                for n in range(2):
                    cols = slice(n * ZERO_ACT, (n + 1) * ZERO_ACT)
                    nc.scalar.copy(agg[:, cols], zero[:].broadcast_to([P, ZERO_ACT])).then_inc(agg_zero, 1)
                    if n == 0:
                        act.wait_ge(src_in, 3 * 16)
                        nc.scalar.copy(src_f[:], src_r[:]).then_inc(src_floated, 1)
                act.wait_ge(src_up, 1)
                nc.scalar.copy(src_idx[:], bank[0][:, 0:TILES]).then_inc(src_idx_made, 1)
                act.wait_ge(src_idx_made, 1)

            @block.gpsimd
            def _(pool):
                nc.gpsimd.iota(iota_i[:], pattern=[[1, P]], base=0, channel_multiplier=0).then_inc(pool_consts, 1)
                nc.gpsimd.iota(col_i[:], pattern=[[1, 1]], base=0, channel_multiplier=1).then_inc(pool_consts, 1)
                nc.gpsimd.memset(agg[:, 2 * ZERO_ACT:], 0.0).then_inc(agg_zero, 1)

            @block.vector
            def _(dve):
                done = [0]

                def step(ins):
                    done[0] += 1
                    ins.then_inc(step_done, 1)
                    dve.wait_ge(step_done, done[0])

                for table, fill in ((dst_r, PAD_NODE), (src_r, 0), (attr_r, 0)):
                    nc.vector.memset(table[96:RT, RC - 1, :], fill).then_inc(rows_padded, 1)
                for cleared in (zero, w_bd, root_bd, center, quarter):
                    nc.vector.memset(cleared[:], 0.0).then_inc(consts_made, 1)
                nc.vector.memset(eps[:], EPS).then_inc(consts_made, 1)
                for a in range(KS):
                    nc.vector.memset(minus_grid[:, a:a + 1], -a / (KS - 1)).then_inc(consts_made, 1)
                dve.wait_ge(consts_made, 5)
                for b in range(4):
                    rows = slice(b * C, (b + 1) * C)
                    nc.vector.memset(center[rows, rows], -1.0 / C).then_inc(consts_made, 1)
                    nc.vector.memset(quarter[rows, b:b + 1], 1.0 / C).then_inc(consts_made, 1)
                dve.wait_ge(pool_consts, 2)
                nc.vector.tensor_copy(iota_row[:], iota_i[:]).then_inc(consts_made, 1)
                nc.vector.tensor_copy(col_f[:], col_i[:]).then_inc(consts_made, 1)
                dve.wait_ge(consts_made, CONSTS - 1)
                nc.vector.tensor_scalar(ident[:], iota_row[:], col_f[:, 0:1], None, ALU.is_equal).then_inc(consts_made, 1)
                dve.wait_ge(consts_made, CONSTS)
                step(nc.vector.tensor_tensor(center[:], center[:], ident[:], ALU.add))
                dve.wait_ge(dst_in, 3 * 16)
                nc.vector.tensor_scalar(sb_i[:], dst_r[:], 8, None, ALU.logical_shift_right)
                nc.vector.tensor_scalar(j_i[:], dst_r[:], 1, None, ALU.bitwise_and)
                step(nc.vector.tensor_scalar(pl_i[:], dst_r[:], 1, P - 1, ALU.logical_shift_right, ALU.bitwise_and))
                nc.vector.tensor_copy(sb_f[:], sb_i[:])
                nc.vector.tensor_copy(pl_f[:], pl_i[:])
                step(nc.vector.tensor_copy(j_f[:], j_i[:]))
                nc.vector.tensor_reduce(low[:], sb_f[:], AX_X, ALU.min)
                nc.vector.scalar_tensor_tensor(out=sb_m[:], in0=sb_f[:], scalar=float(PAD_NODE // SB), in1=sb_f[:],
                                               op0=ALU.is_lt, op1=ALU.mult)
                step(nc.vector.scalar_tensor_tensor(out=blk_f[:], in0=sb_f[:], scalar=float(J), in1=j_f[:],
                                                    op0=ALU.mult, op1=ALU.add))
                nc.vector.tensor_reduce(high[:], sb_m[:], AX_X, ALU.max)
                step(nc.vector.tensor_scalar(low_c[:], low[:], float(NSB - 1), None, ALU.min))
                nc.vector.scalar_tensor_tensor(out=rel_f[:], in0=low_c[:].unsqueeze(2).broadcast_to([RT, RC, P]),
                                               scalar=-float(J), in1=blk_f[:], op0=ALU.mult, op1=ALU.add)
                step(nc.vector.tensor_tensor(span[:], high[:], low_c[:], ALU.subtract))
                assert done[0] == TABLE_STEPS
                dve.wait_ge(attr_up, D)
                for d in range(D):
                    nc.vector.tensor_scalar(attr[:, d, :], bank[(6, 7)[d]][:, 0:TILES], 0.0, 1.0, ALU.max, ALU.min)
                dve.wait_ge(root_up, 1)
                nc.vector.tensor_copy(root_t[:], bank[3][:, 0:P])
                dve.wait_ge(range_up, 1)
                for n, (g0, g1, win) in enumerate(SECTIONS):
                    last = nc.vector.tensor_reduce(span_w[:, n:n + 1], bank[4][0:1, g0 * GT:g1 * GT], AX_X, ALU.max)
                step(last)
                for n, (g0, g1, win) in enumerate(SECTIONS):
                    last = nc.vector.tensor_scalar(span_i[:, n:n + 1], span_w[:, n:n + 1],
                                                   float(-(-(1 << RECIP_SHIFT) // win)), None, ALU.mult)
                step(last)
                step(nc.vector.tensor_scalar(span_s[:], span_i[:], RECIP_SHIFT, None, ALU.arith_shift_right))
                step(nc.vector.tensor_reduce(widest[:], span_s[:], AX_X, ALU.max))
                step(nc.vector.tensor_scalar(sweeps_i[:], widest[:], 1.0, None, ALU.add))
                nc.vector.tensor_copy(base_row[:], bank[5][0:1, 0:TILES])
                dve.wait_ge(tables_up, 2)
                nc.vector.tensor_scalar(minus_plane[:], bank[1][:, 0:TILES], -1.0, None, ALU.mult)
                step(nc.vector.tensor_copy(rel[:], bank[2][:, 0:TILES]))
                dve.wait_ge(agg_zero, 3)

            @block.tensor
            def _(pe):
                pe.wait_ge(consts_made, CONSTS)
                pe.wait_ge(root_in, 4 * 16)
                nc.tensor.transpose(bank[3][:, 0:P], root_bd[:], ident[:]).then_inc(root_up, 1)
                pe.wait_ge(attr_in, 3 * 16)
                for d in range(D):
                    for c in range(RC):
                        last = nc.tensor.transpose(bank[(6, 7)[d]][:, c * RT:(c + 1) * RT],
                                                   attr_r[:, c, :].rearrange("r (p d) -> r p d", d=D)[:, :, d],
                                                   ident[0:RT, 0:RT])
                    last.then_inc(attr_up, 1)
                pe.wait_ge(step_done, TABLE_STEPS)
                for i, row in ((5, low_c), (4, span)):
                    for c in range(RC):
                        last = nc.tensor.transpose(bank[i][0:1, c * RT:(c + 1) * RT], row[:, c:c + 1], ident[0:RT, 0:RT])
                last.then_inc(range_up, 1)
                for i, table in ((1, pl_f), (2, rel_f)):
                    for c in range(RC):
                        last = nc.tensor.transpose(bank[i][:, c * RT:(c + 1) * RT], table[:, c, :], ident[0:RT, 0:RT])
                    last.then_inc(tables_up, 1)
                pe.wait_ge(src_floated, 1)
                for c in range(RC):
                    last = nc.tensor.transpose(bank[0][:, c * RT:(c + 1) * RT], src_f[:, c, :], ident[0:RT, 0:RT])
                last.then_inc(src_up, 1)

        with ExitStack() as st:
            def tmp(name, shape, dt=F32):
                return st.enter_context(nc.sbuf_tensor(name, shape, dt))
            idx_slot = [tmp(f"idx_slot{s}", [P, GT], I32) for s in range(SLOTS)]
            xg = [tmp(f"xg{s}", [P, GT, C]) for s in range(SLOTS)]
            dist = tmp("dist", [P, D, TILES])
            hat = tmp("hat", [P, KS, D, TILES])
            xc = tmp("xc", [P, GT, C])
            xr = [tmp(f"xr{s}", [P, GT, C]) for s in range(2)]
            sq = tmp("sq", [P, GT, C])
            row_sum = tmp("row_sum", [P, GT])
            sq_sum = tmp("sq_sum", [P, GT])
            std = tmp("std", [P, GT])
            rstd = tmp("rstd", [P, GT])
            scaled = tmp("scaled", [P, K, GT])
            spread = [tmp(f"spread{s}", [P, K, GT, C]) for s in range(2)]
            spread_t = [tmp(f"spread_t{s}", [P, K, P]) for s in range(2)]
            msg = [tmp(f"msg{s}", [P, GT, CW]) for s in range(2)]
            away = tmp("away", [P, GT, P])
            onehot = [tmp(f"onehot{s}", [P, GT, P]) for s in range(2)]
            placed = [tmp(f"placed{s}", [P, GT, WB, CW]) for s in range(2)]
            KB = 3
            ps_spread, ps_msg, ps_win = bank[0:3], bank[3], bank[4:8]

            S = {n: sem(n) for n in (
                "idx_ready", "dist_done", "hats_done", "mask_done", "basis_done", "ones_set", "sum_done", "xc_done",
                "sq_done", "relu_done", "sqsum_done", "std_done", "rstd_done", "scaled_done", "spread_done",
                "turned", "turned_out", "msg_made", "msg_out", "away_done", "onehot_done", "placed_done",
                "win_made", "win_added", "moved_on")}
            landed = [sem(f"landed{s}") for s in range(SLOTS)]
            sweep_sems = list(S.values()) + landed

            def win_of(g):
                return next(win for g0, g1, win in SECTIONS if g0 <= g < g1)

            def run_steps(eng, step, drain=True, spare=0):
                def by_hand(g0, g1):
                    for g in range(g0, g1):
                        step(Step(g, g // 4, g % 4, *(win_of(g - lag) if 0 <= g - lag < GRP else None
                                                      for lag in (PLACE_LAG, ADD_LAG))))
                by_hand(0, HEAD)
                at = HEAD
                for n, (its, win) in enumerate(LOOPS):
                    if n:
                        by_hand(at, at + BETWEEN)
                        at += BETWEEN
                    its -= spare if n == len(LOOPS) - 1 else 0
                    assert at % 4 == HEAD % 4
                    with eng.Fori(at // 4, at // 4 + its) as i:
                        for u in range(HEAD % 4, HEAD % 4 + 4):
                            step(Step(i * 4 + u, i + u // 4, u % 4, win, win))
                    at += 4 * its
                by_hand(at, GRP + ADD_LAG if drain else GRP)

            def is_group(g):
                return not isinstance(g, int) or 0 <= g < GRP

            def after(g, n):
                return not isinstance(g, int) or g >= n

            def tiles(g):
                return slice(g * GT, (g + 1) * GT) if isinstance(g, int) else ds(g * GT, GT)

            sweeps = nc.values_load(sweeps_i[0:1, 0:1], min_val=1, max_val=NSB)
            with nc.Fori(0, sweeps):
                with nc.Block() as block:
                    @block.gpsimd
                    def _(pool):
                        def step(s):
                            pool.wait_ge(S["idx_ready"], s.g + 1)
                            pool.nop(nofuse=True)
                            for t in range(GT):
                                nc.gpsimd.indirect_dma_start(
                                    out=xg[s.slot][:, t, :], out_offset=None, in_=x,
                                    in_offset=bass.IndirectOffsetOnAxis(idx_slot[s.slot][:, t:t + 1], 0),
                                ).then_inc(landed[s.slot], 16)
                        run_steps(pool, step, drain=False)

                    @block.scalar
                    def _(act):
                        def give_indices(g, slot):
                            act.wait_ge(S["idx_ready"], g)
                            nc.scalar.copy(idx_slot[slot][:], src_idx[:, tiles(g)]).then_inc(S["idx_ready"], 1)

                        def take_turned(g, h):
                            if after(g, 2):
                                act.wait_ge(S["msg_made"], g - 1)
                            for n in range(K // KB):
                                act.wait_ge(S["turned"], g * (K // KB) + (n + 1))
                                nc.scalar.copy(spread_t[h][:, n * KB:(n + 1) * KB, :],
                                               ps_spread[n][:, 0:KB * P].rearrange("p (k e) -> p k e", k=KB)
                                               ).then_inc(S["turned_out"], 1)

                        def square_relu(g, h):
                            act.wait_ge(S["xc_done"], g + 1)
                            nc.scalar.activation(sq[:], xc[:], ACT.Square).then_inc(S["sq_done"], 1)
                            nc.scalar.activation(xr[h][:], xc[:], ACT.Relu).then_inc(S["relu_done"], 1)

                        def deviation(g):
                            act.wait_ge(S["sqsum_done"], g + 1)
                            nc.scalar.activation(std[:], sq_sum[:], ACT.Sqrt, bias=eps[:, 0:1],
                                                 scale=1.0 / C).then_inc(S["std_done"], 1)

                        def one_hot(g, h):
                            if after(g, 1):
                                act.wait_ge(S["onehot_done"], g)
                            for t in range(GT):
                                at = g * GT + t
                                b = minus_plane[:, at:at + 1] if isinstance(g, int) else minus_plane[:, ds(at, 1)]
                                nc.scalar.activation(away[:, t, :], iota_row[:], ACT.Square, bias=b
                                                     ).then_inc(S["away_done"], 1)
                            if after(g, 2):
                                act.wait_ge(S["win_made"], (g - 1) * GT)
                            act.wait_ge(S["away_done"], (g + 1) * GT)
                            nc.scalar.activation(onehot[h][:], away[:], ACT.Relu, bias=1.0, scale=-1.0
                                                 ).then_inc(S["onehot_done"], 1)

                        def take_messages(g, h):
                            if after(g, 2):
                                act.wait_ge(S["placed_done"], g - 1)
                            act.wait_ge(S["msg_made"], g + 1)
                            nc.scalar.copy(msg[h][:, :, 0:C], ps_msg[:, 0:GT * C].rearrange("p (t c) -> p t c", t=GT)
                                           ).then_inc(S["msg_out"], 1)

                        def step(s):
                            turned = after(s.g, 2) and is_group(s.g - 2)
                            if is_group(s.g):
                                square_relu(s.g, s.slot % 2)
                                if is_group(s.g + SLOTS):
                                    give_indices(s.g + SLOTS, s.slot)
                            if turned:
                                take_turned(s.g - 2, s.slot % 2)
                            if after(s.g, 3) and is_group(s.g - 3):
                                take_messages(s.g - 3, (s.slot - 3) % 2)
                            if is_group(s.g):
                                deviation(s.g)
                            if after(s.g, 3) and is_group(s.g - 3):
                                one_hot(s.g - 3, (s.slot - 3) % 2)

                        for a in range(KS):
                            if a:
                                act.wait_ge(S["hats_done"], a)
                            nc.scalar.activation(dist[:], attr[:], ACT.Abs, bias=minus_grid[:, a:a + 1]
                                                 ).then_inc(S["dist_done"], 1)
                            act.wait_ge(S["dist_done"], a + 1)
                            nc.scalar.activation(hat[:, a, :, :], dist[:], ACT.Relu, bias=1.0, scale=-float(KS - 1)
                                                 ).then_inc(S["hats_done"], 1)
                        run_steps(act, step, spare=1)

                    @block.vector
                    def _(dve):
                        for g in range(SLOTS):
                            nc.vector.tensor_copy(idx_slot[g][:], src_idx[:, tiles(g)]).then_inc(S["idx_ready"], 1)
                        for h in range(2):
                            nc.vector.memset(msg[h][:, :, C:CW], 1.0).then_inc(S["ones_set"], 1)
                        nc.vector.tensor_tensor(
                            mask[:], rel[:].unsqueeze(2).broadcast_to([P, TILES, WB]),
                            iota_row[:, 0:WB].unsqueeze(1).broadcast_to([P, TILES, WB]),
                            ALU.is_equal).then_inc(S["mask_done"], 1)
                        dve.wait_ge(S["hats_done"], KS)
                        for k in range(K):
                            nc.vector.tensor_tensor(basis[:, k, :], hat[:, k // KS, 0, :], hat[:, k % KS, 1, :],
                                                    ALU.mult).then_inc(S["basis_done"], 1)
                        dve.wait_ge(S["basis_done"], K)
                        dve.wait_ge(S["mask_done"], 1)
                        dve.wait_ge(S["ones_set"], 2)

                        def sum_rows(g, turn, slot):
                            dve.wait_ge(landed[slot], turn * (16 * GT) + 16 * GT)
                            nc.vector.tensor_reduce(row_sum[:], xg[slot][:], AX_X, ALU.add).then_inc(S["sum_done"], 1)

                        def center_rows(g, slot):
                            if after(g, 1):
                                dve.wait_ge(S["relu_done"], g)
                            dve.wait_ge(S["sum_done"], g + 1)
                            nc.vector.scalar_tensor_tensor(
                                out=xc[:], in0=row_sum[:].unsqueeze(2).broadcast_to([P, GT, C]),
                                scalar=-1.0 / C, in1=xg[slot][:], op0=ALU.mult, op1=ALU.add).then_inc(S["xc_done"], 1)

                        def place(g, h, win):
                            if after(g, 2):
                                dve.wait_ge(S["win_made"], (g - 1) * GT)
                            dve.wait_ge(S["msg_out"], g + 1)
                            shape = [P, GT, win * J, CW]
                            nc.vector.tensor_tensor(
                                placed[h][:, :, 0:win * J, :],
                                mask[:, tiles(g), 0:win * J].unsqueeze(3).broadcast_to(shape),
                                msg[h][:].unsqueeze(2).broadcast_to(shape), ALU.mult).then_inc(S["placed_done"], 1)

                        def sum_squares(g):
                            dve.wait_ge(S["sq_done"], g + 1)
                            nc.vector.tensor_reduce(sq_sum[:], sq[:], AX_X, ALU.add).then_inc(S["sqsum_done"], 1)

                        def invert_deviation(g):
                            dve.wait_ge(S["std_done"], g + 1)
                            nc.vector.reciprocal(rstd[:], std[:]).then_inc(S["rstd_done"], 1)

                        def scale_basis(g):
                            dve.wait_ge(S["rstd_done"], g + 1)
                            nc.vector.tensor_tensor(scaled[:], basis[:, :, tiles(g)],
                                                    rstd[:].unsqueeze(1).broadcast_to([P, K, GT]),
                                                    ALU.mult).then_inc(S["scaled_done"], 1)

                        def spread_rows(g, h):
                            if after(g, 2):
                                dve.wait_ge(S["turned"], (g - 1) * (K // KB))
                            dve.wait_ge(S["scaled_done"], g + 1)
                            shape = [P, K, GT, C]
                            nc.vector.tensor_tensor(spread[h][:], xr[h][:].unsqueeze(1).broadcast_to(shape),
                                                    scaled[:].unsqueeze(3).broadcast_to(shape), ALU.mult
                                                    ).then_inc(S["spread_done"], 1)

                        def window_starts(g):
                            _, values = nc.values_load_multi_w_load_instructions(
                                base_row[0:1, tiles(g)], engines=[dve.engine], min_val=0, max_val=NSB - 1,
                                skip_runtime_bounds_check_because="made below NSB")
                            return values

                        def add_window(g, t, win, start):
                            if after(g * GT + t, 1):
                                dve.wait_ge(S["win_added"], g * GT + t)
                            a = agg[:, ds(start * BW, win * BW)]
                            nc.vector.tensor_tensor(a, a, ps_win[t][:, 0:win * BW], ALU.add
                                                    ).then_inc(S["win_added"], 1)

                        def step(s):
                            now, add = is_group(s.g), after(s.g, ADD_LAG)
                            spread_now = after(s.g, 1) and is_group(s.g - 1)
                            if after(s.g, PLACE_LAG) and is_group(s.g - PLACE_LAG):
                                place(s.g - PLACE_LAG, (s.slot - PLACE_LAG) % 2, s.place_win)
                            if add:
                                old = s.g - ADD_LAG
                                starts = window_starts(old)
                                dve.wait_ge(S["win_made"], (old + 1) * GT)
                                add_window(old, 0, s.add_win, starts[0])
                            if now:
                                sum_rows(s.g, s.turn, s.slot)
                            if spread_now:
                                invert_deviation(s.g - 1)
                            if add:
                                add_window(old, 1, s.add_win, starts[1])
                            if now:
                                center_rows(s.g, s.slot)
                            if spread_now:
                                scale_basis(s.g - 1)
                            if add:
                                add_window(old, 2, s.add_win, starts[2])
                            if spread_now:
                                spread_rows(s.g - 1, (s.slot - 1) % 2)
                            if now:
                                sum_squares(s.g)
                            if add:
                                add_window(old, 3, s.add_win, starts[3])
                        run_steps(dve, step)
                        dve.wait_ge(S["win_added"], TILES)
                        for g0, g1, win in SECTIONS:
                            cols = slice(g0 * GT, g1 * GT)
                            nc.vector.tensor_scalar(rel[:, cols], rel[:, cols], -float(win * J), None, ALU.add
                                                    ).then_inc(S["moved_on"], 1)
                            nc.vector.tensor_scalar(base_row[:, cols], base_row[:, cols], float(win), float(NSB - 1),
                                                    ALU.add, ALU.min).then_inc(S["moved_on"], 1)
                        dve.wait_ge(S["moved_on"], 2 * len(SECTIONS))

                    @block.tensor
                    def _(pe):
                        def turn_spread(g, h):
                            if after(g, 1):
                                pe.wait_ge(S["turned_out"], g * (K // KB))
                            pe.wait_ge(S["spread_done"], g + 1)
                            for k in range(K):
                                last = nc.tensor.transpose(ps_spread[k // KB][:, k % KB * P:(k % KB + 1) * P],
                                                           spread[h][:, k, :, :].rearrange("p t c -> p (t c)"), ident[:])
                                if k % KB == KB - 1:
                                    last.then_inc(S["turned"], 1)

                        def make_messages(g, h):
                            if after(g, 1):
                                pe.wait_ge(S["msg_out"], g)
                            pe.wait_ge(S["turned_out"], (g + 1) * (K // KB))
                            for k in range(K):
                                last = nc.tensor.matmul(ps_msg[:, 0:GT * C], spread_t[h][:, k, :], w_bd[:, k, :],
                                                        start=(k == 0), stop=(k == K - 1))
                            last.then_inc(S["msg_made"], 1)

                        def make_windows(g, h, win):
                            pe.wait_ge(S["onehot_done"], g + 1)
                            pe.wait_ge(S["placed_done"], g + 1)
                            for t in range(GT):
                                if after(g, 1):
                                    pe.wait_ge(S["win_added"], (g - 1) * GT + (t + 1))
                                nc.tensor.matmul(ps_win[t][:, 0:win * BW], onehot[h][:, t, :],
                                                 placed[h][:, t, 0:win * J, :].rearrange("p w c -> p (w c)"),
                                                 start=True, stop=True).then_inc(S["win_made"], 1)

                        def step(s):
                            if after(s.g, 3) and is_group(s.g - 3):
                                make_messages(s.g - 3, (s.slot - 3) % 2)
                            if after(s.g, PLACE_LAG) and is_group(s.g - PLACE_LAG):
                                make_windows(s.g - PLACE_LAG, (s.slot - PLACE_LAG) % 2, s.place_win)
                            if after(s.g, 1) and is_group(s.g - 1):
                                turn_spread(s.g - 1, (s.slot - 1) % 2)

                        pe.wait_ge(weights_in, 64)
                        run_steps(pe, step, drain=False)
                        assert PLACE_LAG == 4
                        last = GRP - 1
                        make_messages(last - 2, (last - 2) % 2)
                        make_windows(last - 3, (last - 3) % 2, win_of(last - 3))
                        turn_spread(last, last % 2)
                        make_messages(last - 1, (last - 1) % 2)
                        make_windows(last - 2, (last - 2) % 2, win_of(last - 2))
                        make_messages(last, last % 2)
                        make_windows(last - 1, (last - 1) % 2, win_of(last - 1))
                        make_windows(last, last % 2, win_of(last))

                nums = sorted(s.num for s in sweep_sems)
                assert nums == list(range(nums[0], nums[0] + len(nums)))
                nc.gpsimd.dma_reset(range(nums[0], nums[-1] + 1))
                nc.gpsimd.sem_clear(range(nums[0], nums[-1] + 1))
                nc.all_engine_barrier()

        with ExitStack() as st:
            def tmp(name, shape, dt=F32):
                return st.enter_context(nc.sbuf_tensor(name, shape, dt))
            xb = tmp("xb", [P, 2, CC])
            x_t = tmp("x_t", [P, 2, CC])
            relu_t = tmp("relu_t", [P, 2, CC])
            sq_t = tmp("sq_t", [P, 2, CC])
            nstd = tmp("nstd", [P, 2, CB])
            nrstd = tmp("nrstd", [P, 2, CB])
            deg = tmp("deg", [P, 2, CB])
            rdeg = tmp("rdeg", [P, 2, CB])
            mean_msg = tmp("mean_msg", [P, 2, CC])
            part = tmp("part", [P, 2, CC])
            part2 = tmp("part2", [P, 2, CC])
            res = tmp("res", [P, 2, CC])
            ps_xt, ps_xc, ps_root, ps_var = bank[0:2], bank[2:4], bank[4:6], bank[6:8]
            stored = [sem(f"stored{s}") for s in range(2)]
            T = {n: sem("n_" + n) for n in (
                "xt", "xt_out", "xc", "relu", "sq", "var", "root", "std", "rstd", "xb", "deg", "rdeg",
                "mean", "part", "part2", "res")}
            assert (NCH - 9) % 4 == 0
            NL = (NCH - 9) // 4

            def tail_view(a):
                return a[full_sb * SB:N, :].rearrange("(p j) c -> p (j c)", j=J)

            block = st.enter_context(nc.Block())

            def run_chunks(eng, step):
                for c in range(4):
                    step(c, 0, c)
                with eng.Fori(0, NL) as i:
                    for u in range(4):
                        step(i * 4 + (4 + u), i + 1, u)
                for c in range(NCH - 5, NCH):
                    step(c, c // 4, c % 4)

            def cut(a, c, n):
                return a[:, c * n:(c + 1) * n] if isinstance(c, int) else a[:, ds(c * n, n)]

            def first_is(c, n):
                return isinstance(c, int) and c < n

            @block.sync
            def _(sp):
                views, out_views = chunk_view(x), chunk_view(out)
                LAST = NCH - 1

                def rows(view, c):
                    return view[:, c * CS:(c + 1) * CS, :] if isinstance(c, int) else view[:, ds(c * CS, CS), :]

                def load(c, slot):
                    sp.wait_ge(T["xt"], c - (XBUF - 1))
                    sp.wait_ge(T["xb"], c - (XBUF - 1))
                    if isinstance(c, int) and c == LAST:
                        sp.dma_start(xin[:, slot, 0:tail_sb * J * C].rearrange("p (s e) -> p s e", s=tail_sb),
                                     views[:, c * CS:c * CS + tail_sb, :]).then_inc(x_in[slot], 16)
                        sp.dma_start(xin[0:tail_nodes // J, slot, tail_sb * J * C:(tail_sb + 1) * J * C],
                                     tail_view(x)).then_inc(x_in[slot], 16)
                    else:
                        sp.dma_start(xin[:, slot, :].rearrange("p (s e) -> p s e", s=CS),
                                     rows(views, c)).then_inc(x_in[slot], 16)

                def store(c, h):
                    sp.wait_ge(T["res"], c + 1)
                    if isinstance(c, int) and c == LAST:
                        sp.dma_start(views_tail(out_views), res[:, h, 0:tail_sb * J * C].rearrange(
                            "p (s e) -> p s e", s=tail_sb)).then_inc(stored[h], 16)
                        sp.dma_start(tail_view(out), res[0:tail_nodes // J, h, tail_sb * J * C:(tail_sb + 1) * J * C]
                                     ).then_inc(stored[h], 16)
                    else:
                        sp.dma_start(rows(out_views, c), res[:, h, :].rearrange("p (s e) -> p s e", s=CS)
                                     ).then_inc(stored[h], 16)

                def views_tail(view):
                    return view[:, LAST * CS:LAST * CS + tail_sb, :]

                with sp.Fori(0, (NCH - 5) // 4) as i:
                    for u in range(4):
                        load(i * 4 + (4 + u), u)
                        store(i * 4 + u, u % 2)
                load(LAST, LAST % XBUF)
                for c in range(NCH - 5, NCH):
                    store(c, c % 2)
                sp.wait_ge(stored[0], 16 * (NCH // 2) + 32)
                sp.wait_ge(stored[1], 16 * (NCH // 2))

            def landed_count(c, turn):
                return turn * 16 + (32 if first_is(c, NCH) and c == NCH - 1 else 16)

            @block.gpsimd
            def _(pool):
                pool.wait_ge(bias_in, 16)

                def step(c, turn, slot):
                    h = slot % 2
                    pool.wait_ge(x_in[slot], landed_count(c, turn))
                    nc.gpsimd.tensor_tensor(xb[:, h, :].rearrange("p (b c) -> p b c", c=C),
                                            xin[:, slot, :].rearrange("p (b c) -> p b c", c=C),
                                            bias[:].unsqueeze(1).broadcast_to([P, CB, C]), ALU.add).then_inc(T["xb"], 1)
                    pool.wait_ge(T["xb"], c + 1)
                    if not first_is(c, 2):
                        pool.wait_ge(T["res"], c - 1)
                    pool.wait_ge(T["mean"], c + 1)
                    nc.gpsimd.tensor_tensor(part2[:, h, :], mean_msg[:, h, :], xb[:, h, :], ALU.add).then_inc(T["part2"], 1)
                run_chunks(pool, step)

            @block.tensor
            def _(pe):
                def turn_in(c, turn, slot):
                    h = slot % 2
                    pe.wait_ge(x_in[slot], landed_count(c, turn))
                    if not first_is(c, 2):
                        pe.wait_ge(T["xt_out"], c - 1)
                    for q in range(QUADS):
                        last = nc.tensor.transpose(ps_xt[h][:, q * P:(q + 1) * P], xin[:, slot, q * P:(q + 1) * P], ident[:])
                    last.then_inc(T["xt"], 1)

                def centre(c, h):
                    if not first_is(c, 2):
                        pe.wait_ge(T["relu"], c - 1)
                    pe.wait_ge(T["xt_out"], c + 1)
                    nc.tensor.matmul(ps_xc[h][:], center[:], x_t[:, h, :], start=True, stop=True).then_inc(T["xc"], 1)

                def variance(c, h):
                    if not first_is(c, 2):
                        pe.wait_ge(T["std"], c - 1)
                    pe.wait_ge(T["sq"], c + 1)
                    for q in range(QUADS):
                        last = nc.tensor.matmul(ps_var[h][:, q * 4:(q + 1) * 4], sq_t[:, h, q * P:(q + 1) * P], quarter[:],
                                                start=True, stop=True)
                    last.then_inc(T["var"], 1)

                def root_product(c, h):
                    if not first_is(c, 2):
                        pe.wait_ge(T["part"], c - 1)
                    pe.wait_ge(T["relu"], c + 1)
                    for q in range(QUADS):
                        last = nc.tensor.matmul(ps_root[h][:, q * P:(q + 1) * P], relu_t[:, h, q * P:(q + 1) * P], root_t[:],
                                                start=True, stop=True)
                    last.then_inc(T["root"], 1)

                def step(c, turn, slot):
                    h = slot % 2
                    centre(c, h)
                    if not first_is(c, 1):
                        root_product(c - 1, 1 - h)
                    if not (isinstance(c, int) and c == NCH - 1):
                        turn_in(c + 1, turn + (slot + 1) // 4, (slot + 1) % 4)
                    variance(c, h)
                turn_in(0, 0, 0)
                run_chunks(pe, step)
                root_product(NCH - 1, (NCH - 1) % 2)

            @block.scalar
            def _(act):
                def copy_turned(c, h):
                    if not first_is(c, 2):
                        act.wait_ge(T["xc"], c - 1)
                    act.wait_ge(T["xt"], c + 1)
                    nc.scalar.copy(x_t[:, h, :], ps_xt[h][:]).then_inc(T["xt_out"], 1)

                def step(c, turn, slot):
                    h = slot % 2
                    if not first_is(c, 2):
                        act.wait_ge(T["root"], c - 1)
                        act.wait_ge(T["var"], c - 1)
                    act.wait_ge(T["xc"], c + 1)
                    nc.scalar.activation(sq_t[:, h, :], ps_xc[h][:], ACT.Square).then_inc(T["sq"], 1)
                    nc.scalar.activation(relu_t[:, h, :], ps_xc[h][:], ACT.Relu).then_inc(T["relu"], 1)
                    if not (isinstance(c, int) and c == NCH - 1):
                        copy_turned(c + 1, 1 - h)
                    if not first_is(c, 2):
                        act.wait_ge(T["rstd"], c - 1)
                    act.wait_ge(T["var"], c + 1)
                    nc.scalar.activation(nstd[:, h, :], ps_var[h][:, 0:CB], ACT.Sqrt, bias=eps[:, 0:1]).then_inc(T["std"], 1)
                copy_turned(0, 0)
                run_chunks(act, step)

            @block.vector
            def _(dve):
                agg_blocks = agg[:].rearrange("p (b e) -> p b e", e=CW)
                cols = lambda a, h: a[:, h, :].rearrange("p (b c) -> p b c", c=C)

                def agg_of(c):
                    return agg_blocks[:, c * CB:(c + 1) * CB, :] if isinstance(c, int) else (
                        cut(agg[:], c, CB * CW).rearrange("p (b e) -> p b e", e=CW))

                def degree(c, h):
                    if not first_is(c, 2):
                        dve.wait_ge(T["rdeg"], c - 1)
                    nc.vector.tensor_scalar(deg[:, h, :], agg_of(c)[:, :, C], 1.0, None, ALU.max).then_inc(T["deg"], 1)

                def invert_degree(c, h):
                    if not first_is(c, 2):
                        dve.wait_ge(T["mean"], c - 1)
                    dve.wait_ge(T["deg"], c + 1)
                    nc.vector.reciprocal(rdeg[:, h, :], deg[:, h, :]).then_inc(T["rdeg"], 1)

                def mean_message(c, h):
                    if not first_is(c, 2):
                        dve.wait_ge(T["part2"], c - 1)
                    dve.wait_ge(T["rdeg"], c + 1)
                    nc.vector.tensor_tensor(cols(mean_msg, h), agg_of(c)[:, :, 0:C],
                                            rdeg[:, h, :].unsqueeze(2).broadcast_to([P, CB, C]),
                                            ALU.mult).then_inc(T["mean"], 1)

                def result(c, turn, slot, h):
                    if not first_is(c, 2):
                        dve.wait_ge(stored[h], turn * 32 + 16 * (slot // 2))
                    dve.wait_ge(T["part"], c + 1)
                    dve.wait_ge(T["part2"], c + 1)
                    nc.vector.tensor_tensor(res[:, h, :], part[:, h, :], part2[:, h, :], ALU.add).then_inc(T["res"], 1)

                def step(c, turn, slot):
                    h = slot % 2
                    not_last = not (isinstance(c, int) and c == NCH - 1)
                    mean_message(c, h)
                    if not_last:
                        degree(c + 1, 1 - h)
                    if not first_is(c, 1):
                        result(c - 1, turn, slot - 1, 1 - h)
                    if not_last:
                        invert_degree(c + 1, 1 - h)
                    dve.wait_ge(T["std"], c + 1)
                    nc.vector.reciprocal(nrstd[:, h, :], nstd[:, h, :]).then_inc(T["rstd"], 1)
                    if not first_is(c, 2):
                        dve.wait_ge(T["res"], c - 1)
                    dve.wait_ge(T["rstd"], c + 1)
                    dve.wait_ge(T["root"], c + 1)
                    nc.vector.tensor_tensor(cols(part, h), ps_root[h][:].rearrange("p (b c) -> p b c", c=C),
                                            nrstd[:, h, :].unsqueeze(2).broadcast_to([P, CB, C]),
                                            ALU.mult).then_inc(T["part"], 1)
                degree(0, 0)
                invert_degree(0, 0)
                run_chunks(dve, step)
                result(NCH - 1, (NCH - 1) // 4, (NCH - 1) % 4, (NCH - 1) % 2)


_INS = ['x', 'src', 'dst', 'edge_attr_2', 'L0_gnn_weight', 'L0_gnn_root_w', 'L0_gnn_root_b']
_OUTS = [((100000, 32), 'float32')]


def kernel(**inputs):
    import numpy as _np
    import concourse.bacc as _bacc
    from concourse import mybir as _mybir
    from concourse.bass_utils import run_bass_kernel_spmd as _run

    nc = _bacc.Bacc("TRN2", target_bir_lowering=False, num_devices=1)
    arrays, args = {}, []
    for name in _INS:
        a = _np.ascontiguousarray(inputs[name])
        arrays[f"in_{name}_dram"] = a
        args.append(nc.dram_tensor(f"in_{name}_dram", a.shape, _mybir.dt.from_np(a.dtype), kind="ExternalInput").ap())
    for i, (shape, dtype) in enumerate(_OUTS):
        dt = _mybir.dt.from_np(_np.dtype(dtype))
        args.append(nc.dram_tensor(f"out_{i}_dram", shape, dt, kind="ExternalOutput").ap())
    build_gnn(nc, *args)
    r = _run(nc, [arrays], core_ids=[0])
    return r.results[0]["out_0_dram"]
```
